# Optimizing a Trainium2 kernel written in Bass

```python
import numpy as np
import jax
import jax.numpy as jnp

def _softmax(x, axis=-1):
    return jax.nn.softmax(x, axis=axis)

def _gelu(x):
    return jax.nn.gelu(x, approximate=True)

def _silu(x):
    return jax.nn.silu(x)

def _sigmoid(x):
    return jax.nn.sigmoid(x)

def _layernorm(x, axis=-1, eps=1e-05):
    m = jnp.mean(x, axis=axis, keepdims=True)
    v = jnp.var(x, axis=axis, keepdims=True)
    return (x - m) / jnp.sqrt(v + eps)

def _scatter_add(tgt, idx, src, axis=0):
    return tgt.at[idx].add(src)

def _segment_sum(src, seg, n):
    return jax.ops.segment_sum(src, seg, n)
kernel_name = 'mk_adj_ffn_d1_adj_r2_7d1583'

def setup_inputs(seed: int=0):
    np.random.seed(seed)
    _w = jnp.asarray

    def _rec_inputs():
        import jax
        import jax.numpy as jnp
        _gk = jax.random.key(seed)
        x = -0.0005207 + 1.001 * jax.random.normal(jax.random.fold_in(_gk, 1), (2048, 256), jnp.float32)
        _a = jax.random.bernoulli(jax.random.fold_in(_gk, 2), 0.00195312, (2048, 2048))
        _a = jnp.logical_or(_a, jnp.swapaxes(_a, -1, -2))
        _a = jnp.logical_or(_a, jnp.eye(2048, dtype=bool))
        adj = _a.astype(jnp.int32)
        _nm = jnp.ones((2048,), dtype=bool)
        nodemask = jnp.where(_nm, 1.0, 0.0).astype(jnp.int32)
        return (x, adj, nodemask)
    x, adj, nodemask = _rec_inputs()

    def _L0_gnn_setup():
        import jax, jax.numpy as jnp
        import numpy as np
        D = 256
        H = 8
        HD = D // H
        EPS = 1e-05
        NEG = -1e+30

        def layer_norm(x, scale, bias):
            mu = jnp.mean(x, axis=-1, keepdims=True)
            var = jnp.mean(jnp.square(x - mu), axis=-1, keepdims=True)
            return (x - mu) * jax.lax.rsqrt(var + EPS) * scale + bias
        key = jax.random.key(seed)
        ks = jax.random.split(key, 16)
        S = T = 2048
        inp = {'h_source': jax.random.normal(ks[0], (S, D), jnp.float32), 'h_target': jax.random.normal(ks[1], (T, D), jnp.float32), 'edge_mask': jax.random.randint(ks[2], (T, S), 0, 2, jnp.int32), 'source_mask': jnp.ones((S,), jnp.int32), 'target_mask': jnp.ones((T,), jnp.int32), 'ln1_scale': jnp.ones((D,), jnp.float32), 'ln1_bias': jnp.zeros((D,), jnp.float32), 'Wq': jax.random.normal(ks[3], (D, D), jnp.float32) / np.sqrt(D), 'bq': jnp.zeros((D,), jnp.float32), 'Wk': jax.random.normal(ks[4], (D, D), jnp.float32) / np.sqrt(D), 'bk': jnp.zeros((D,), jnp.float32), 'Wv': jax.random.normal(ks[5], (D, D), jnp.float32) / np.sqrt(D), 'bv': jnp.zeros((D,), jnp.float32), 'Wo': jax.random.normal(ks[6], (D, D), jnp.float32) / np.sqrt(D), 'bo': jnp.zeros((D,), jnp.float32), 'ln2_scale': jnp.ones((D,), jnp.float32), 'ln2_bias': jnp.zeros((D,), jnp.float32), 'W1': jax.random.normal(ks[7], (D, 4 * D), jnp.float32) / np.sqrt(D), 'W2': jax.random.normal(ks[8], (4 * D, D), jnp.float32) / np.sqrt(4 * D)}
        return inp
    _L0_gnn_all = _L0_gnn_setup()
    _L0_gnn_in = {k: v for k, v in _L0_gnn_all.items() if k in ('h_target', 'ln1_scale', 'ln1_bias', 'Wq', 'bq', 'Wk', 'bk', 'Wv', 'bv', 'Wo', 'bo', 'ln2_scale', 'ln2_bias', 'W1', 'W2')}
    del _L0_gnn_all

    def _L0_ffn_setup():
        import jax, jax.numpy as jnp
        import numpy as np
        import math
        B, T, D = (4, 4096, 256)
        E, K, F = (8, 2, 1024)
        CAP_FACTOR = 1.25
        key = jax.random.key(seed)
        ks = jax.random.split(key, 4)
        return {'x': jax.random.normal(ks[0], (B, T, D), jnp.float32), 'gate_w': jax.random.normal(ks[1], (E, D), jnp.float32) * 0.01, 'w1': jax.random.normal(ks[2], (E, D, F), jnp.float32) * (1.0 / np.sqrt(D)), 'b1': jnp.zeros((E, F), jnp.float32), 'w2': jax.random.normal(ks[3], (E, F, D), jnp.float32) * (1.0 / np.sqrt(F)), 'b2': jnp.zeros((E, D), jnp.float32)}
    _L0_ffn_all = _L0_ffn_setup()
    _L0_ffn_in = {k: v for k, v in _L0_ffn_all.items() if k in ('gate_w', 'w1', 'b1', 'w2', 'b2')}
    del _L0_ffn_all
    return {'x': x, 'adj': adj, 'nodemask': nodemask, 'L0_gnn_h_target': _L0_gnn_in['h_target'], 'L0_gnn_ln1_scale': _L0_gnn_in['ln1_scale'], 'L0_gnn_ln1_bias': _L0_gnn_in['ln1_bias'], 'L0_gnn_Wq': _L0_gnn_in['Wq'], 'L0_gnn_bq': _L0_gnn_in['bq'], 'L0_gnn_Wk': _L0_gnn_in['Wk'], 'L0_gnn_bk': _L0_gnn_in['bk'], 'L0_gnn_Wv': _L0_gnn_in['Wv'], 'L0_gnn_bv': _L0_gnn_in['bv'], 'L0_gnn_Wo': _L0_gnn_in['Wo'], 'L0_gnn_bo': _L0_gnn_in['bo'], 'L0_gnn_ln2_scale': _L0_gnn_in['ln2_scale'], 'L0_gnn_ln2_bias': _L0_gnn_in['ln2_bias'], 'L0_gnn_W1': _L0_gnn_in['W1'], 'L0_gnn_W2': _L0_gnn_in['W2'], 'L0_ffn_gate_w': _L0_ffn_in['gate_w'], 'L0_ffn_w1': _L0_ffn_in['w1'], 'L0_ffn_b1': _L0_ffn_in['b1'], 'L0_ffn_w2': _L0_ffn_in['w2'], 'L0_ffn_b2': _L0_ffn_in['b2']}

def reference(x, adj, nodemask, L0_gnn_h_target, L0_gnn_ln1_scale, L0_gnn_ln1_bias, L0_gnn_Wq, L0_gnn_bq, L0_gnn_Wk, L0_gnn_bk, L0_gnn_Wv, L0_gnn_bv, L0_gnn_Wo, L0_gnn_bo, L0_gnn_ln2_scale, L0_gnn_ln2_bias, L0_gnn_W1, L0_gnn_W2, L0_ffn_gate_w, L0_ffn_w1, L0_ffn_b1, L0_ffn_w2, L0_ffn_b2):
    import jax
    import jax.numpy as jnp

    def _L0_gnn_ref(h_source, h_target, edge_mask, source_mask, target_mask, ln1_scale, ln1_bias, Wq, bq, Wk, bk, Wv, bv, Wo, bo, ln2_scale, ln2_bias, W1, W2):
        import jax, jax.numpy as jnp
        import numpy as np
        D = 256
        H = 8
        HD = D // H
        EPS = 1e-05
        NEG = -1e+30

        def layer_norm(x, scale, bias):
            mu = jnp.mean(x, axis=-1, keepdims=True)
            var = jnp.mean(jnp.square(x - mu), axis=-1, keepdims=True)
            return (x - mu) * jax.lax.rsqrt(var + EPS) * scale + bias
        smask = (source_mask == 1)[:, None]
        tmask = (target_mask == 1)[:, None]
        hs = layer_norm(h_source, ln1_scale, ln1_bias)
        ht = layer_norm(h_target, ln1_scale, ln1_bias)
        hs = jnp.where(smask, hs, 0.0)
        ht = jnp.where(tmask, ht, 0.0)
        T, S = (ht.shape[0], hs.shape[0])
        q = (ht @ Wq + bq).reshape(T, H, HD) / jnp.sqrt(jnp.float32(HD))
        k = (hs @ Wk + bk).reshape(S, H, HD)
        v = (hs @ Wv + bv).reshape(S, H, HD)
        logits = jnp.einsum('thd,shd->hts', q, k)
        logits = jnp.where(edge_mask[None] != 0, logits, NEG)
        probs = jax.nn.softmax(logits, axis=-1)
        ctx = jnp.einsum('hts,shd->thd', probs, v).reshape(T, D)
        attn = ctx @ Wo + bo
        attn = jnp.where(tmask, attn, 0.0)
        ht = ht + attn
        ht = layer_norm(ht, ln2_scale, ln2_bias)
        ht = jnp.where(tmask, ht, 0.0)
        ff = jax.nn.gelu(ht @ W1) @ W2
        return ht + ff

    def _L0_ffn_ref(x, gate_w, w1, b1, w2, b2):
        import jax, jax.numpy as jnp
        import numpy as np
        import math
        B, T, D = (4, 4096, 256)
        E, K, F = (8, 2, 1024)
        CAP_FACTOR = 1.25
        Bx, Tx, Dx = x.shape
        N = Bx * Tx
        C = math.ceil(CAP_FACTOR * N / E)
        xf = x.reshape(N, Dx)
        probs = jax.nn.softmax(xf @ gate_w.T, axis=-1)
        topk_vals, topk_idx = jax.lax.top_k(probs, K)
        topk_vals = topk_vals / topk_vals.sum(-1, keepdims=True)
        flat_e = topk_idx.reshape(N * K)
        onehot = jax.nn.one_hot(flat_e, E, dtype=jnp.int32)
        pos = jnp.cumsum(onehot, axis=0)[jnp.arange(N * K), flat_e] - 1
        keep = pos < C
        pos_safe = jnp.where(keep, pos, C)
        token_ids = jnp.repeat(jnp.arange(N), K)
        buf = jnp.zeros((E, C + 1, Dx), x.dtype).at[flat_e, pos_safe].set(xf[token_ids])
        expert_in = buf[:, :C]
        h = jax.nn.gelu(jnp.einsum('ecd,edf->ecf', expert_in, w1) + b1[:, None, :], approximate=False)
        expert_out = jnp.einsum('ecf,efd->ecd', h, w2) + b2[:, None, :]
        gathered = expert_out[flat_e, jnp.minimum(pos_safe, C - 1)]
        w = (topk_vals.reshape(N * K) * keep).astype(x.dtype)
        out = (gathered * w[:, None]).reshape(N, K, Dx).sum(axis=1)
        return out.reshape(Bx, Tx, Dx)
    x = x + _L0_gnn_ref(_layernorm(x, axis=-1), L0_gnn_h_target, adj, nodemask, nodemask, L0_gnn_ln1_scale, L0_gnn_ln1_bias, L0_gnn_Wq, L0_gnn_bq, L0_gnn_Wk, L0_gnn_bk, L0_gnn_Wv, L0_gnn_bv, L0_gnn_Wo, L0_gnn_bo, L0_gnn_ln2_scale, L0_gnn_ln2_bias, L0_gnn_W1, L0_gnn_W2)
    x = x + _L0_ffn_ref(_layernorm(x, axis=-1)[None], L0_ffn_gate_w, L0_ffn_w1, L0_ffn_b1, L0_ffn_w2, L0_ffn_b2)[0]
    return x

_drawn_inputs = setup_inputs


def setup_inputs(seed=0):
    import zlib

    import numpy as np

    out = dict(_drawn_inputs(seed))
    spreads = {'L0_gnn_ln1_scale': (1.0, 0.2),
     'L0_gnn_ln1_bias': (0.0, 0.1),
     'L0_gnn_bq': (0.0, 0.1),
     'L0_gnn_bk': (0.0, 0.8),
     'L0_gnn_bv': (0.0, 0.1),
     'L0_gnn_bo': (0.0, 0.1),
     'L0_gnn_ln2_scale': (1.0, 0.2),
     'L0_gnn_ln2_bias': (0.0, 0.1),
     'L0_ffn_b1': (0.0, 0.436),
     'L0_ffn_b2': (0.0, 0.304)}
    factors = {}
    for name, (base, spread) in spreads.items():
        noise = np.random.default_rng([zlib.crc32(name.encode()), seed]).standard_normal(out[name].shape)
        drawn = base * np.exp(spread * noise) if base else spread * noise
        out[name] = jnp.asarray(drawn.astype(out[name].dtype))
    for name, factor in factors.items():
        out[name] = (out[name] * factor).astype(out[name].dtype)
    return out
```

```python
from contextlib import ExitStack

import concourse.bass as bass
import concourse.mybir as mybir

F32 = mybir.dt.float32
F16 = mybir.dt.float16
BF16 = mybir.dt.bfloat16
I32 = mybir.dt.int32
ALU = mybir.AluOpType
ACT = mybir.ActivationFunctionType
AX_X = mybir.AxisListType.X

P = 128
EPS = 1e-5
BIG = 1e30
AHEAD_QK = 3
RING = 4
UNITS = 16


def evacuated_by(k, g):
    return "act" if g in (0, 2) or (g == 1 and k % 2 == 0) else "dve"


def evac_count(engine, it, k, g):
    pair = {"act": 5, "dve": 3}[engine]
    within = sum(evacuated_by(kk, gg) == engine
                 for kk in range(k % 2 + 1) for gg in range(4) if (kk, gg) <= (k % 2, g))
    return it * (pair * UNITS // 2) + (k // 2) * pair + within


def wait(eng, sem, value):
    if not isinstance(value, int) or value > 0:
        eng.wait_ge(sem, value)


def peeled(eng, n):
    def run(body):
        body(0)
        with eng.Fori(1, n) as i:
            body(i)
    return run


def hold(eng, sem, value, passed):
    wait(eng, sem, value)
    eng.sem_inc(passed, 1)


def build(nc, x, adj, nodemask, h_target, ln1_scale, ln1_bias, Wq, bq, Wk, bk, Wv, bv, Wo, bo,
          ln2_scale, ln2_bias, W1, W2, gate_w, w1, b1, w2, b2, out):
    N, D = x.shape
    H, HD = 8, D // 8
    NT = N // P
    ND = D // P
    F = W1.shape[1]
    NF = F // P
    E, NFE = w1.shape[0], w1.shape[2] // P
    CAP = -(-5 * N // (4 * E))
    SLOTS = E * CAP
    ROWS = [P, P, CAP - 2 * P]
    NG = 4
    GT = NT // NG
    GW = GT * P
    ROUNDS = NT * H // UNITS
    HG = 4
    SCALE = 1.0 / float(HD) ** 0.5
    FAR = float(1 << 20)
    assert GW == 512 and NT == 16 and 4 * HD == P and UNITS == 2 * H

    slots_in = nc.dram_tensor("slots_in", (SLOTS, D), F32, kind="Internal").ap()
    slots_out = nc.dram_tensor("slots_out", (SLOTS, D), F32, kind="Internal").ap()

    with ExitStack() as ctx:
        def sb(name, shape, dt=F32):
            return ctx.enter_context(nc.sbuf_tensor(name, shape, dt))

        def sem(name):
            return ctx.enter_context(nc.semaphore(name))

        ps = ctx.enter_context(nc.psum_tensor("ps", [P, 8, 512], F32))

        xn = sb("xn", [P, NT, D])
        ht = sb("ht", [P, NT, D])
        vals = sb("vals", [P, NT, D])
        keys_q_arena = sb("keys_q_arena", [P, 16384])
        work = sb("work", [P, 12800])
        wqkvo = sb("wqkvo", [P, 4, ND, D])
        w1_sb = sb("w1_sb", [P, ND, F])
        adj_sb = sb("adj_sb", [P, N], I32)
        mask_sb = [sb(f"mask{i}", [P, N], BF16) for i in range(2)]
        rows_sb = sb("rows_sb", [P, 6, D])
        ident = sb("ident", [P, P])
        fold = sb("fold", [P, HD])
        before = sb("before", [P, P])
        ones = sb("ones", [P, P])
        lower = sb("lower", [P, E, E])
        first_slot = sb("first_slot", [P, E])
        cols = sb("cols", [P, 4, ND])
        nm_i = sb("nm_i", [NT, P], I32)
        nm_f = sb("nm_f", [NT, P])
        nmask = sb("nmask", [P, NT])
        gw_rows = sb("gw_rows", [E, D])
        gwT = sb("gwT", [P, ND, E])
        b1_rows = sb("b1_rows", [E * NFE, P])
        b1T = sb("b1T", [P, E * NFE])
        stats = sb("stats", [P, 2 * NT, 6])
        mean = sb("mean", [P, 2 * NT])
        tmpa = sb("tmpa", [P, 2 * NT])
        tmpb = sb("tmpb", [P, 2 * NT])
        vare = sb("vare", [P, 2 * NT])
        sdev = sb("sdev", [P, 2 * NT])
        rstd = sb("rstd", [P, 2 * NT])
        least = sb("least", [P, 2, UNITS])
        rowsum = sb("rowsum", [P, UNITS])
        rinv = sb("rinv", [P, 2, H])

        def view(arena, at, words, dt=F32):
            a = arena[:, at:at + words]
            return a if dt == F32 else a.bitcast(dt)

        kst = view(keys_q_arena, 0, 8192, F16).rearrange("p (h n) -> p h n", h=H)
        qst = view(keys_q_arena, 8192, 8192, F16).rearrange("p (h n) -> p h n", h=H)
        hsT = view(work, 0, 1024).rearrange("p (k n) -> p k n", k=ND)
        htT = view(work, 1024, 1024).rearrange("p (k n) -> p k n", k=ND)
        q_f = view(work, 2048, 1024).rearrange("p (k n) -> p k n", k=ND)
        k_f = view(work, 3072, 1024).rearrange("p (k n) -> p k n", k=ND)
        split = [view(work, 4096 + 2048 * i, 2048, F16).rearrange("p (k n) -> p k n", k=ND)
                 for i in range(4)]
        logits = [view(work, 2048 * i, 2048) for i in range(RING)]
        probsT = [view(work, 8192 + 2048 * i, 2048) for i in range(2)]
        ctx_part = view(work, 12288, 512)
        hs_c, ht_c = w1_sb[:, 0, :].rearrange("p (j d) -> p j d", j=GT), w1_sb[:, 1, :].rearrange("p (j d) -> p j d", j=GT)
        cx_c = view(work, 0, 1024).rearrange("p (j d) -> p j d", j=GT)

        x2 = view(keys_q_arena, 0, 4096).rearrange("p (t d) -> p t d", t=NT)
        w2_sb = view(keys_q_arena, 4096, 2048).rearrange("p (k d) -> p k d", k=NF)
        ctxT = view(keys_q_arena, 6144, 1024).rearrange("p (k n) -> p k n", k=ND)
        hid = view(keys_q_arena, 7168, 4096).rearrange("p (f n) -> p f n", f=NF)
        u_c = view(keys_q_arena, 11264, 1024).rearrange("p (j d) -> p j d", j=GT)
        uT = view(keys_q_arena, 12288, 1024).rearrange("p (k n) -> p k n", k=ND)
        xn3_c = view(keys_q_arena, 13312, 1024).rearrange("p (j d) -> p j d", j=GT)
        xn3T = view(keys_q_arena, 14336, 1024).rearrange("p (k n) -> p k n", k=ND)
        gates = view(keys_q_arena, 15360, NT * E).rearrange("p (t e) -> p t e", t=NT)
        big3 = [view(work, 1024 * i, 1024).rearrange("p (t a b) -> p t a b", t=NT, a=E) for i in range(2)]
        small = [view(work, 2048 + 128 * i, 128).rearrange("p (t e) -> p t e", t=NT) for i in range(12)]
        tiny = [view(work, 3584 + 16 * i, 16) for i in range(16)]
        idx_out = [view(work, 3840 + 16 * i, 16, I32) for i in range(2)]
        idx_in = [view(work, 3872 + 16 * i, 16, I32) for i in range(2)]
        ew1 = [view(work, 4096 + 2048 * i, 2048).rearrange("p (k f) -> p k f", k=ND) for i in range(2)]
        ew2 = [view(work, 8192 + 2048 * i, 2048).rearrange("p (k d) -> p k d", k=NFE) for i in range(2)]
        xin = [view(keys_q_arena, 11968 + 768 * i, 768).rearrange("p (j d) -> p j d", j=3) for i in range(2)]
        xinT = view(keys_q_arena, 4096, 640).rearrange("p (k n) -> p k n", k=ND)
        ehid = [view(keys_q_arena, 4736 + 2560 * i, 2560).rearrange("p (f n) -> p f n", f=NFE)
                for i in range(2)]
        eout = [view(keys_q_arena, 9856 + 768 * i, 768).rearrange("p (j d) -> p j d", j=3) for i in range(2)]
        b2_row = [view(keys_q_arena, 11392 + 256 * i, 256) for i in range(2)]
        b1_e = [view(keys_q_arena, 11904 + 8 * i, 8) for i in range(2)]
        got = [xn, ht]

        x_in = [sem(f"x_in{g}") for g in range(NG)]
        ht_in = [sem(f"ht_in{g}") for g in range(NG)]
        w_in, small_in, zero_done = map(sem, ("w_in", "small_in", "zero_done"))
        consts, gp_step, adj_zeroed = map(sem, ("consts", "gp_step", "adj_zeroed"))
        ln_step, sqrt_done = sem("ln_step"), sem("sqrt_done")
        prep_dve, prep_pe = sem("prep_dve"), sem("prep_pe")
        x_scaled, norm_x_step = sem("x_scaled"), sem("norm_x_step")
        hs_ready, ht_ready, norm_t_step = sem("hs_ready"), sem("ht_ready"), sem("norm_t_step")
        htT_psum, hsT_psum, htT_out, hsT_out = map(sem, ("htT_psum", "hsT_psum", "htT_out", "hsT_out"))
        q_psum, k_psum, v_psum, q_out, k_out, v_out = map(
            sem, ("q_psum", "k_psum", "v_psum", "q_out", "k_out", "v_out"))
        split_step, split_done, stacked = sem("split_step"), sem("split_done"), sem("stacked")
        adj_in, mask_ready, mask_used = sem("adj_in"), sem("mask_ready"), sem("mask_used")
        scores, masked = sem("scores"), sem("masked")
        exp_done, turned = sem("exp_done"), sem("turned")
        pool_passed, dve_passed = sem("pool_passed"), sem("dve_passed")
        evac = {"act": sem("evac_act"), "dve": sem("evac_dve")}
        pv_done, part_out, folded = sem("pv_done"), sem("part_out"), sem("folded")
        rinv_done, ctx_ready = sem("rinv_done"), sem("ctx_ready")
        w2_in, x2_in = sem("w2_in"), sem("x2_in")
        cx_copied, cxT_psum, cxT_out, wo_psum, ffn_step, u_ready = map(
            sem, ("cx_copied", "cxT_psum", "cxT_out", "wo_psum", "ffn_step", "u_ready"))
        uT_psum, uT_out, h_psum, h_out, y_psum, xn3_ready = map(
            sem, ("uT_psum", "uT_out", "h_psum", "h_out", "y_psum", "xn3_ready"))
        n3T_psum, n3T_out, gate_psum, gate_out = map(sem, ("n3T_psum", "n3T_out", "gate_psum", "gate_out"))
        sqrt_c, route_step, gate_exp, sel_ready, pos_psum = map(
            sem, ("sqrt_c", "route_step", "gate_exp", "sel_ready", "pos_psum"))
        routed, scattered = sem("routed"), sem("scattered")
        ew_in, xin_in, b2_in, eo_stored = ([sem(f"{name}{i}") for i in range(2)]
                                           for name in ("ew_in", "xin_in", "b2_in", "eo_stored"))
        xinT_psum, xinT_out, eh_psum, eh_out, eo_psum, eo_out, b1_ready = map(
            sem, ("xinT_psum", "xinT_out", "eh_psum", "eh_out", "eo_psum", "eo_out", "b1_ready"))
        gathered = [sem(f"gathered{g}") for g in range(NG)]
        mixed, mix_step, stored = sem("mixed"), sem("mix_step"), sem("stored")

        def moments(v, n, st, base):
            m, a, b, ve, r = mean[:, 0:n], tmpa[:, 0:n], tmpb[:, 0:n], vare[:, 0:n], rstd[:, 0:n]
            v.tensor_tensor(m, st[:, :, 1], st[:, :, 4], ALU.add).then_inc(ln_step, 1)
            v.tensor_tensor(a, st[:, :, 1], st[:, :, 4], ALU.subtract).then_inc(ln_step, 1)
            v.tensor_tensor(b, st[:, :, 2], st[:, :, 5], ALU.add).then_inc(ln_step, 1)
            v.wait_ge(ln_step, base + 3)
            v.tensor_scalar(m, m, 0.5, None, ALU.mult).then_inc(ln_step, 1)
            v.scalar_tensor_tensor(out=ve, in0=a, scalar=0.25, in1=a, op0=ALU.mult, op1=ALU.mult).then_inc(ln_step, 1)
            v.wait_ge(ln_step, base + 5)
            v.scalar_tensor_tensor(out=a, in0=b, scalar=1.0 / D, in1=ve, op0=ALU.mult, op1=ALU.add).then_inc(ln_step, 1)
            v.wait_ge(ln_step, base + 6)
            v.tensor_scalar(ve, a, EPS, None, ALU.add).then_inc(ln_step, 1)

        def inverse_root(v, n, base, root_sem, root_count):
            a, ve, r = tmpa[:, 0:n], vare[:, 0:n], rstd[:, 0:n]
            v.wait_ge(root_sem, root_count)
            v.reciprocal(r, sdev[:, 0:n]).then_inc(ln_step, 1)
            v.wait_ge(ln_step, base + 8)
            v.tensor_tensor(a, r, r, ALU.mult).then_inc(ln_step, 1)
            v.wait_ge(ln_step, base + 9)
            v.tensor_tensor(a, a, ve, ALU.mult).then_inc(ln_step, 1)
            v.wait_ge(ln_step, base + 10)
            v.tensor_scalar(a, a, -0.5, 1.5, ALU.mult, ALU.add).then_inc(ln_step, 1)
            v.wait_ge(ln_step, base + 11)
            v.tensor_tensor(r, r, a, ALU.mult).then_inc(ln_step, 1)
            v.wait_ge(ln_step, base + 12)

        LN_STEPS = 12
        LN_BEFORE = 32 + LN_STEPS + 16 + LN_STEPS
        LN_CHUNK = 2 * (GT + LN_STEPS)
        DVE_CHUNK = 4 + 4 + 3 + 2 + 4

        def rounds(eng, body):
            body(0, True, False)
            with eng.Fori(1, ROUNDS - 1) as it:
                body(it, False, False)
            body(ROUNDS - 1, False, True)

        block = ctx.enter_context(nc.Block())

        @block.sync
        def _(sp):
            for dst, src, s in ((ht, h_target, ht_in), (xn, x, x_in)):
                for g in range(NG):
                    sp.dma_start(dst[:, g * GT:(g + 1) * GT, :],
                                 src[g * GW:(g + 1) * GW, :].rearrange("(j p) d -> p j d", p=P)).then_inc(s[g], 16)
            sp.dma_start(nm_i[:, :], nodemask.rearrange("(t p) -> t p", p=P)).then_inc(small_in, 16)
            sp.dma_start(gw_rows[:, :], gate_w[:, :]).then_inc(small_in, 16)
            sp.dma_start(b1_rows[:, :], b1.rearrange("e (f p) -> (e f) p", p=P)).then_inc(small_in, 16)
            for i, r in enumerate((bq, bk)):
                sp.dma_start(cols[:, i, :], r.rearrange("(c p) -> p c", p=P), allow_slow_non_contiguous=True).then_inc(small_in, 16)
            for i, r in enumerate((ln1_scale, ln1_bias, bv, bo, ln2_scale, ln2_bias)):
                sp.dma_start(rows_sb[:, i, :], r.partition_broadcast(P)).then_inc(small_in, 16)
            for i, w in enumerate((Wq, Wk, Wv, Wo)):
                sp.dma_start(wqkvo[:, i, :, :], w.rearrange("(k p) n -> p k n", p=P)).then_inc(w_in, 16)
            sp.wait_ge(adj_zeroed, 1)
            zeros = slots_in.rearrange("(p r) d -> p (r d)", p=P)
            for at in range(0, SLOTS * D // P, N // 2):
                sp.dma_start(zeros[:, at:at + N // 2], adj_sb[:, 0:N // 2].bitcast(F32)).then_inc(zero_done, 16)

            with sp.Fori(0, NG) as g:
                sp.wait_ge(split_done, 2 * g + 2)
                for dst, parts in ((qst, (0, 0, 1, 1)), (kst, (2, 3, 2, 3))):
                    for hq in range(4):
                        for slot, part in enumerate(parts):
                            sp.dma_start(
                                dst[HD * slot:HD * (slot + 1), hq:H:4, bass.ds(g * GW, GW)],
                                split[part][HD * hq:HD * (hq + 1), :, bass.ds(g * GW, GW)]).then_inc(stacked, 16)

            sp.wait_ge(htT_psum, NG)
            sp.wait_ge(hsT_psum, NG)
            sp.dma_start(w1_sb[:, :, :], W1.rearrange("(k p) n -> p k n", p=P)).then_inc(w2_in, 16)
            sp.wait_ge(zero_done, 16 * (SLOTS * D // P // (N // 2)))
            sp.dma_start(adj_sb[:, :], adj[0:P, :]).then_inc(adj_in, 16)
            with sp.Fori(1, NT) as t:
                sp.wait_ge(mask_ready, t)
                sp.dma_start(adj_sb[:, :], adj[bass.ds(t * P, P), :]).then_inc(adj_in, 16)

            sp.wait_ge(ctx_ready, NT)
            sp.dma_start(x2[:, :, :], x.rearrange("(t p) d -> p t d", p=P)).then_inc(x2_in, 16)
            sp.dma_start(w2_sb[:, :, :], W2.rearrange("(k p) n -> p k n", p=P)).then_inc(w2_in, 16)

            sp.wait_ge(routed, 1)
            def load_expert(e, i):
                sp.dma_start(ew1[i], w1[bass.ds(e, 1), :, :].rearrange("e (k p) f -> p (e k) f", p=P)).then_inc(ew_in[i], 16)
                sp.dma_start(ew2[i], w2[bass.ds(e, 1), :, :].rearrange("e (k p) f -> p (e k) f", p=P)).then_inc(ew_in[i], 16)
                sp.dma_start(b2_row[i], b2[bass.ds(e, 1), :].rearrange("e d -> (e d)").partition_broadcast(P)).then_inc(b2_in[i], 16)
                sp.dma_start(xin[i][:, 0:2, :],
                             slots_in[bass.ds(e * CAP, 2 * P), :].rearrange("(j p) d -> p j d", p=P)).then_inc(xin_in[i], 16)
                sp.dma_start(xin[i][0:ROWS[2], 2, :],
                             slots_in[bass.ds(e * CAP + 2 * P, ROWS[2]), :]).then_inc(xin_in[i], 16)

            sp.wait_ge(scattered, 16 * 2 * NT)
            load_expert(0, 0)
            load_expert(1, 1)
            with sp.Fori(1, E // 2) as pair:
                for i in range(2):
                    sp.wait_ge(eo_psum, 2 * pair + i - 1)
                    sp.wait_ge(eo_out, 2 * pair + i - 1)
                    load_expert(pair * 2 + i, i)

            with sp.Fori(0, NG) as g:
                sp.wait_ge(mixed, GT * g + GT)
                sp.dma_start(out[bass.ds(g * GW, GW), :].rearrange("(j p) d -> p j d", p=P),
                             x2[:, bass.ds(g * GT, GT), :]).then_inc(stored, 16)
            sp.wait_ge(stored, 16 * NG)

        @block.gpsimd
        def _(pool):
            pool.memset(adj_sb[:, 0:N // 2], 0).then_inc(adj_zeroed, 1)
            pool.memset(ident[:, :], 0.0).then_inc(gp_step, 1)
            pool.memset(fold[:, :], 0.0).then_inc(gp_step, 1)
            pool.memset(before[:, :], 1.0).then_inc(gp_step, 1)
            pool.memset(lower[:, :, :], 1.0).then_inc(gp_step, 1)
            pool.memset(ones[:, :], 1.0).then_inc(consts, 1)
            pool.iota(first_slot[:, :], [[CAP, E]], base=0, channel_multiplier=0,
                      allow_small_or_imprecise_dtypes=True).then_inc(consts, 1)
            pool.wait_ge(gp_step, 4)
            pool.affine_select(out=ident[:, :], in_=ident[:, :], compare_op=ALU.not_equal, fill=1.0,
                               base=0, pattern=[[-1, P]], channel_multiplier=1).then_inc(consts, 1)
            pool.affine_select(out=before[:, :], in_=before[:, :], compare_op=ALU.is_gt, fill=0.0,
                               base=0, pattern=[[1, P]], channel_multiplier=-1).then_inc(consts, 1)
            pool.affine_select(out=lower[:, :, :], in_=lower[:, :, :], compare_op=ALU.is_gt, fill=0.0,
                               base=0, pattern=[[1, E], [-1, E]], channel_multiplier=0).then_inc(consts, 1)
            for j in range(P // HD):
                pool.affine_select(out=fold[:, :], in_=fold[:, :], compare_op=ALU.not_equal, fill=1.0,
                                   base=-HD * j, pattern=[[-1, HD]], channel_multiplier=1).then_inc(gp_step, 1)
                pool.wait_ge(gp_step, 5 + j)
            pool.wait_ge(small_in, 16 * 11)
            pool.wait_ge(prep_dve, 3)
            @peeled(pool, NG)
            def _(g):
                hold(pool, x_scaled, GT * g + GT, pool_passed)
                src = xn[:, bass.ds(g * GT, GT), :]
                pool.tensor_tensor(src, src, rows_sb[:, 0, :].unsqueeze(1).broadcast_to((P, GT, D)), ALU.mult)\
                    .then_inc(norm_x_step, 1)
                hold(pool, norm_x_step, 2 * g + 1, pool_passed)
                pool.tensor_tensor(src, src, rows_sb[:, 1, :].unsqueeze(1).broadcast_to((P, GT, D)), ALU.add)\
                    .then_inc(norm_x_step, 1)
                pool.wait_ge(norm_x_step, 2 * g + 2)
                hold(pool, hsT_psum, g, pool_passed)
                pool.tensor_tensor(hs_c[:, :, :], src,
                                   nmask[:, bass.ds(g * GT, GT)].unsqueeze(2).broadcast_to((P, GT, D)), ALU.mult)\
                    .then_inc(hs_ready, 1)
            for m in range(2):
                pool.wait_ge(adj_in, 16 * (m + 1))
                pool.tensor_scalar(mask_sb[m][:, :], adj_sb[:, :], 0.0, BIG, ALU.is_equal, ALU.mult).then_inc(mask_ready, 1)
            with pool.Fori(1, NT // 2) as pair:
                for m in range(2):
                    pool.wait_ge(adj_in, 32 * pair + 16 * m + 16)
                    hold(pool, mask_used, 2 * pair + m - 1, pool_passed)
                    pool.tensor_scalar(mask_sb[m][:, :], adj_sb[:, :], 0.0, BIG, ALU.is_equal, ALU.mult)\
                        .then_inc(mask_ready, 1)
            @peeled(pool, NG)
            def _(c):
                pool.wait_ge(ctx_ready, NT)
                hold(pool, cxT_psum, c, pool_passed)
                pool.tensor_copy(cx_c, xn[:, bass.ds(c * GT, GT), :]).then_inc(cx_copied, 1)
            pool.wait_ge(routed, 1)
            for t in range(NT):
                for k in range(2):
                    pool.indirect_dma_start(out=slots_in, out_offset=bass.IndirectOffsetOnAxis(idx_out[k][:, t:t + 1], 0),
                                            in_=vals[:, t, :], in_offset=None, bounds_check=SLOTS - 1,
                                            oob_is_err=False).then_inc(scattered, 16)
            for i in range(2):
                pool.wait_ge(eo_stored[i], 32 * E // 2)
            for t in range(NT):
                for k in range(2):
                    pool.indirect_dma_start(out=got[k][:, t, :], out_offset=None, in_=slots_out,
                                            in_offset=bass.IndirectOffsetOnAxis(idx_in[k][:, t:t + 1], 0))\
                        .then_inc(gathered[t // GT], 16)

        @block.scalar
        def _(act):
            act.wait_ge(ln_step, 32 + 7)
            act.activation(sdev[:, 0:2 * NT], vare[:, 0:2 * NT], ACT.Sqrt).then_inc(sqrt_done, 1)
            act.wait_ge(ln_step, 32 + LN_STEPS + 16 + 7)
            act.activation(sdev[:, 0:NT], vare[:, 0:NT], ACT.Sqrt).then_inc(sqrt_done, 1)
            act.wait_ge(prep_dve, 6)
            with act.Fori(0, NG) as g:
                act.wait_ge(htT_psum, g + 1)
                act.activation(htT[:, :, :], ps[:, 0:2, :], ACT.Copy).then_inc(htT_out, 1)
                act.wait_ge(hsT_psum, g + 1)
                act.activation(hsT[:, :, :], ps[:, 2:4, :], ACT.Copy).then_inc(hsT_out, 1)
                act.wait_ge(q_psum, g + 1)
                for c in range(ND):
                    act.activation(q_f[:, c, :], ps[:, 4 + c, :], ACT.Identity, bias=cols[:, 2, c:c + 1],
                                   scale=-SCALE).then_inc(q_out, 1)
                act.wait_ge(k_psum, g + 1)
                for c in range(ND):
                    act.activation(k_f[:, c, :], ps[:, 6 + c, :], ACT.Identity, bias=cols[:, 1, c:c + 1])\
                        .then_inc(k_out, 1)

            def exponentials(it, k):
                n, s = it * UNITS + k, k % UNITS
                wait(act, masked, 2 * n + 2)
                if s % H == 0:
                    wait(act, ctx_ready, it * 2 + k // H - 1)
                act.activation(logits[s % RING], logits[s % RING], ACT.Exp, bias=least[:, 1, s:s + 1], scale=-1.0,
                               accum_out=rowsum[:, s:s + 1]).then_inc(exp_done, 1)

            def copy_out(it, k, g):
                n = it * UNITS + k
                if g == 0:
                    wait(act, pv_done, n - 1)
                wait(act, turned, 4 * n + g + 1)
                act.activation(probsT[k % 2][:, g * 512:(g + 1) * 512], ps[:, 4 + g % 2, :], ACT.Copy)\
                   .then_inc(evac["act"], 1)

            def partial_contexts(it, k):
                G = it * (UNITS // HG) + (k - 5) // HG
                wait(act, pv_done, G * HG + HG)
                wait(act, folded, G)
                act.activation(ctx_part, ps[:, 6, :], ACT.Copy).then_inc(part_out, 1)

            def act_round(it, first, last):
                for k in range(UNITS):
                    if k % HG == 1 and not (first and k < 5):
                        partial_contexts(it, k)
                    if not (last and k + 1 >= UNITS):
                        exponentials(it, k + 1)
                    for g in range(4):
                        if evacuated_by(k, g) == "act":
                            copy_out(it, k, g)

            exponentials(0, 0)
            rounds(act, act_round)
            partial_contexts(ROUNDS, 1)

            with act.Fori(0, NG) as c:
                act.wait_ge(cxT_psum, c + 1)
                act.activation(ctxT[:, :, :], ps[:, 0:2, :], ACT.Copy).then_inc(cxT_out, 1)
                act.wait_ge(ln_step, LN_BEFORE + c * LN_CHUNK + GT + 7)
                act.activation(sdev[:, 0:GT], vare[:, 0:GT], ACT.Sqrt).then_inc(sqrt_c, 1)
                act.wait_ge(uT_psum, c + 1)
                act.activation(uT[:, :, :], ps[:, 0:2, :], ACT.Copy).then_inc(uT_out, 1)
                for f in range(NF):
                    act.wait_ge(h_psum, c * NF + f + 1)
                    act.activation(hid[:, f, :], ps[:, 4 + f % 4, :], ACT.Gelu_apprx_tanh).then_inc(h_out, 1)
                act.wait_ge(ln_step, LN_BEFORE + c * LN_CHUNK + GT + LN_STEPS + GT + 7)
                act.activation(sdev[:, 0:GT], vare[:, 0:GT], ACT.Sqrt).then_inc(sqrt_c, 1)
                act.wait_ge(n3T_psum, c + 1)
                act.activation(xn3T[:, :, :], ps[:, 0:2, :], ACT.Copy).then_inc(n3T_out, 1)

            act.wait_ge(route_step, 1)
            act.activation(small[1], small[0], ACT.Exp).then_inc(gate_exp, 1)

            with act.Fori(0, E // 2) as pair:
                for i in range(2):
                    act.wait_ge(xinT_psum, pair * 2 + i + 1)
                    act.activation(xinT[:, :, :], ps[:, 0:2, 0:CAP], ACT.Copy).then_inc(xinT_out, 1)
                    act.wait_ge(b1_ready, pair * 2 + i + 1)
                    for f in range(NFE):
                        act.wait_ge(eh_psum, (pair * 2 + i) * NFE + f + 1)
                        act.activation(ehid[i][:, f, :], ps[:, 2 + f % 4, 0:CAP], ACT.Gelu,
                                       bias=b1_e[i][:, f:f + 1]).then_inc(eh_out, 1)
                    act.wait_ge(eo_out, pair * 2 + i + 1)
                    act.dma_start(slots_out[bass.ds((pair * 2 + i) * CAP, 2 * P), :].rearrange("(j p) d -> p j d", p=P),
                                  eout[i][:, 0:2, :]).then_inc(eo_stored[i], 16)
                    act.dma_start(slots_out[bass.ds((pair * 2 + i) * CAP + 2 * P, ROWS[2]), :],
                                  eout[i][0:ROWS[2], 2, :]).then_inc(eo_stored[i], 16)

        @block.vector
        def _(v):
            for first, rows_in, arrived in ((0, ht, ht_in), (NT, xn, x_in)):
                for t in range(NT):
                    if t % GT == 0:
                        v.wait_ge(arrived[t // GT], 16)
                    v.bn_stats(stats[:, first + t, :], rows_in[:, t, :]).then_inc(ln_step, 1)
            v.wait_ge(ln_step, 32)
            moments(v, 2 * NT, stats, 32)
            v.wait_ge(small_in, 16 * 11)
            v.tensor_scalar(nm_f[:, :], nm_i[:, :], 1.0, None, ALU.is_equal).then_inc(prep_dve, 1)
            v.tensor_scalar(cols[:, 2, :], cols[:, 0, :], -SCALE, None, ALU.mult).then_inc(prep_dve, 1)
            v.wait_ge(prep_pe, 1)
            v.tensor_copy(nmask[:, :], ps[:, 0, 0:NT]).then_inc(prep_dve, 1)
            v.wait_ge(prep_pe, 2)
            v.tensor_copy(gwT[:, :, :], ps[:, 1, 0:ND * E].rearrange("p (k e) -> p k e", k=ND)).then_inc(prep_dve, 1)
            v.wait_ge(prep_pe, 3)
            v.tensor_copy(b1T[:, :], ps[:, 2, 0:E * NFE]).then_inc(prep_dve, 1)
            inverse_root(v, 2 * NT, 32, sqrt_done, 1)
            v.tensor_copy(tmpb[:, 0:1], rstd[:, 0:1]).then_inc(prep_dve, 1)
            with v.Fori(0, NG) as g:
                for j in range(GT):
                    t = xn[:, bass.ds(g * GT + j, 1), :]
                    v.tensor_scalar(t, t, mean[:, bass.ds(NT + g * GT + j, 1)], rstd[:, bass.ds(NT + g * GT + j, 1)],
                                    ALU.subtract, ALU.mult).then_inc(norm_t_step, 1)
                hold(v, norm_t_step, GT * g + GT, dve_passed)
                for j in range(GT):
                    v.bn_stats(stats[:, bass.ds(NT + g * GT + j, 1), :], xn[:, bass.ds(g * GT + j, 1), :]).then_inc(ln_step, 1)
            with v.Fori(0, NG) as g:
                for j in range(GT):
                    t = ht[:, bass.ds(g * GT + j, 1), :]
                    v.tensor_scalar(t, t, mean[:, bass.ds(g * GT + j, 1)], rstd[:, bass.ds(g * GT + j, 1)],
                                    ALU.subtract, ALU.mult).then_inc(norm_t_step, 1)
            v.wait_ge(norm_t_step, 2 * NT)
            v.wait_ge(ln_step, 32 + LN_STEPS + 16)
            moments(v, NT, stats[:, NT:2 * NT, :], 32 + LN_STEPS + 16)
            inverse_root(v, NT, 32 + LN_STEPS + 16, sqrt_done, 2)
            with v.Fori(0, NG) as g:
                for j in range(GT):
                    t = xn[:, bass.ds(g * GT + j, 1), :]
                    v.tensor_scalar(t, t, mean[:, bass.ds(g * GT + j, 1)], rstd[:, bass.ds(g * GT + j, 1)],
                                    ALU.subtract, ALU.mult).then_inc(x_scaled, 1)
            T0 = 2 * NT
            @peeled(v, NG)
            def _(g):
                t = ht[:, bass.ds(g * GT, GT), :]
                v.tensor_tensor(t, t, rows_sb[:, 0, :].unsqueeze(1).broadcast_to((P, GT, D)), ALU.mult).then_inc(norm_t_step, 1)
                v.wait_ge(norm_t_step, T0 + 3 * g + 1)
                v.tensor_tensor(t, t, rows_sb[:, 1, :].unsqueeze(1).broadcast_to((P, GT, D)), ALU.add).then_inc(norm_t_step, 1)
                v.wait_ge(norm_t_step, T0 + 3 * g + 2)
                v.tensor_tensor(t, t, nmask[:, bass.ds(g * GT, GT)].unsqueeze(2).broadcast_to((P, GT, D)), ALU.mult)\
                    .then_inc(norm_t_step, 1)
                v.wait_ge(norm_t_step, T0 + 3 * g + 3)
                hold(v, htT_psum, g, dve_passed)
                v.tensor_copy(ht_c[:, :, :], t).then_inc(ht_ready, 1)
                for src, hi, lo, done in ((q_f, split[0], split[1], q_out), (k_f, split[2], split[3], k_out)):
                    hold(v, done, ND * g + ND, dve_passed)
                    hi_g, lo_g = hi[:, :, bass.ds(g * GW, GW)], lo[:, :, bass.ds(g * GW, GW)]
                    v.tensor_copy(hi_g, src[:, :, :]).then_inc(split_step, 1)
                    v.wait_ge(split_step, 2 * g + (1 if done is q_out else 2))
                    v.tensor_tensor(lo_g, src[:, :, :], hi_g, ALU.subtract).then_inc(split_done, 1)
                for j in range(2):
                    v.wait_ge(v_psum, 2 * g + j + 1)
                    v.tensor_tensor(vals[:, bass.ds(g * GT + 2 * j, 2), :],
                                    ps[:, j, :].rearrange("p (j d) -> p j d", j=2),
                                    rows_sb[:, 2, :].unsqueeze(1).broadcast_to((P, 2, D)), ALU.add).then_inc(v_out, 1)

            def mask_and_reduce(it, k, half):
                n, s = it * UNITS + k, k % UNITS
                if half == 0:
                    wait(v, turned, 4 * (n - RING) + 4)
                    if s % H == 0:
                        wait(v, mask_ready, it * 2 + k // H + 1)
                else:
                    wait(v, masked, 2 * n + 1)
                hold(v, scores, 2 * n + half + 1, dve_passed)
                view3 = (lambda a: a[:, half * 1024:(half + 1) * 1024].rearrange("p (b n) -> p b n", b=2))
                v.tensor_tensor_reduce(
                    out=view3(logits[s % RING]), in0=ps[:, 2 * half:2 * half + 2, :],
                    in1=view3(mask_sb[s // H]), scale=1.0, scalar=3.0e38 if half == 0 else least[:, 0, s:s + 1],
                    op0=ALU.add, op1=ALU.min, accum_out=least[:, half, s:s + 1]).then_inc(masked, 1)

            def copy_out(it, k, g):
                n = it * UNITS + k
                wait(v, pv_done, n - 1)
                wait(v, turned, 4 * n + g + 1)
                v.tensor_copy(probsT[k % 2][:, g * 512:(g + 1) * 512], ps[:, 4 + g % 2, :]).then_inc(evac["dve"], 1)

            def normalise(it, k):
                t, par = it * 2 + (k - 11) // H, ((k - 11) // H) % 2
                wait(v, folded, 2 * t + 2)
                wait(v, exp_done, 8 * t + 8)
                v.reciprocal(rinv[:, par, :], rowsum[:, par * H:par * H + H]).then_inc(rinv_done, 1)
                wait(v, rinv_done, t + 1)
                dst = xn[:, bass.ds(t, 1), :] if not isinstance(t, int) else xn[:, t:t + 1, :]
                v.tensor_tensor(dst.rearrange("p a (h d) -> p (a h) d", h=H),
                                ps[:, 7, 0:D].rearrange("p (h d) -> p h d", h=H),
                                rinv[:, par, :].unsqueeze(2).broadcast_to((P, H, HD)), ALU.mult).then_inc(ctx_ready, 1)

            def dve_round(it, first, last):
                for k in range(UNITS):
                    ahead = not (last and k + 2 >= UNITS)
                    if ahead:
                        mask_and_reduce(it, k + 2, 0)
                    if evacuated_by(k, 1) == "dve":
                        copy_out(it, k, 1)
                    if ahead:
                        mask_and_reduce(it, k + 2, 1)
                    if (k + 2) % H == H - 1 and ahead:
                        wait(v, masked, 2 * (it * UNITS + k + 2) + 2)
                        v.sem_inc(mask_used, 1)
                    copy_out(it, k, 3)
                    if k % H == 3 and not (first and k < 11):
                        normalise(it, k)

            for k in range(2):
                for half in range(2):
                    mask_and_reduce(0, k, half)
            rounds(v, dve_round)
            normalise(ROUNDS, 3)

            v.wait_ge(x2_in, 16)
            with v.Fori(0, NG) as c:
                step = c * DVE_CHUNK
                tile = bass.ds(c * GT, GT)
                nm = nmask[:, tile].unsqueeze(2).broadcast_to((P, GT, D))
                row = lambda i: rows_sb[:, i, :].unsqueeze(1).broadcast_to((P, GT, D))
                attn = ps[:, 2:4, :].rearrange("p b (j d) -> p (b j) d", j=2)
                v.wait_ge(wo_psum, c + 1)
                v.tensor_tensor(u_c, attn, row(3), ALU.add).then_inc(ffn_step, 1)
                v.wait_ge(ffn_step, step + 1)
                v.tensor_tensor(u_c, u_c, nm, ALU.mult).then_inc(ffn_step, 1)
                v.wait_ge(ffn_step, step + 2)
                v.tensor_tensor(u_c, u_c, ht[:, tile, :], ALU.add).then_inc(ffn_step, 1)
                v.wait_ge(ffn_step, step + 3)
                base = LN_BEFORE + c * LN_CHUNK
                for j in range(GT):
                    v.bn_stats(stats[:, j, :], u_c[:, j, :]).then_inc(ln_step, 1)
                v.wait_ge(ln_step, base + GT)
                moments(v, GT, stats[:, 0:GT, :], base + GT)
                inverse_root(v, GT, base + GT, sqrt_c, c * 2 + 1)
                for j in range(GT):
                    v.tensor_scalar(u_c[:, j, :], u_c[:, j, :], mean[:, j:j + 1], rstd[:, j:j + 1],
                                    ALU.subtract, ALU.mult).then_inc(ffn_step, 1)
                v.wait_ge(ffn_step, step + 7)
                v.tensor_tensor(u_c, u_c, row(4), ALU.mult).then_inc(ffn_step, 1)
                v.wait_ge(ffn_step, step + 8)
                v.tensor_tensor(u_c, u_c, row(5), ALU.add).then_inc(ffn_step, 1)
                v.wait_ge(ffn_step, step + 9)
                v.tensor_tensor(u_c, u_c, nm, ALU.mult).then_inc(u_ready, 1)
                v.wait_ge(u_ready, c + 1)
                v.tensor_tensor(x2[:, tile, :], x2[:, tile, :], u_c, ALU.add).then_inc(ffn_step, 1)
                v.wait_ge(ffn_step, step + 10)
                v.wait_ge(y_psum, c + 1)
                v.tensor_tensor(x2[:, tile, :], attn, x2[:, tile, :], ALU.add).then_inc(ffn_step, 1)
                hold(v, ffn_step, step + 11, dve_passed)
                base = base + GT + LN_STEPS
                for j in range(GT):
                    v.bn_stats(stats[:, j:j + 1, :], x2[:, bass.ds(c * GT + j, 1), :]).then_inc(ln_step, 1)
                v.wait_ge(ln_step, base + GT)
                moments(v, GT, stats[:, 0:GT, :], base + GT)
                inverse_root(v, GT, base + GT, sqrt_c, c * 2 + 2)
                for j in range(GT):
                    v.tensor_scalar(xn3_c[:, j:j + 1, :], x2[:, bass.ds(c * GT + j, 1), :], mean[:, j:j + 1],
                                    rstd[:, j:j + 1], ALU.subtract, ALU.mult).then_inc(xn3_ready, 1)
                hold(v, xn3_ready, c * GT + GT, dve_passed)
                v.tensor_copy(vals[:, tile, :], xn3_c[:, :, :]).then_inc(ffn_step, 1)
                hold(v, gate_psum, c + 1, dve_passed)
                v.tensor_copy(gates[:, tile, :], ps[:, 2, 0:GT * E].rearrange("p (j e) -> p j e", j=GT))\
                    .then_inc(gate_out, 1)
                for j in range(DVE_CHUNK - 12):
                    v.sem_inc(ffn_step, 1)

            count = [1]

            def link(ins, inc=route_step):
                count[0] += 1
                ins.then_inc(inc, 1)
                v.wait_ge(inc, count[0])

            v.wait_ge(gate_out, NG)
            z, ex, rank, w, sel, pos, keep, slot, pick, prod = small[0:10]
            top, total, inv, chosen, kept = tiny[0:5]
            weight = tiny[5:7]
            b16 = lambda a: a.unsqueeze(2).broadcast_to((P, NT, E))
            v.tensor_reduce(top, gates, AX_X, ALU.max).then_inc(mix_step, 1)
            v.wait_ge(mix_step, 1)
            v.tensor_tensor(z, gates, b16(top), ALU.subtract).then_inc(route_step, 1)
            v.wait_ge(route_step, 1)
            other = gates.unsqueeze(2).broadcast_to((P, NT, E, E))
            own = gates.unsqueeze(3).broadcast_to((P, NT, E, E))
            link(v.tensor_tensor(big3[0], other, own, ALU.is_gt))
            link(v.tensor_tensor(big3[1], other, own, ALU.is_equal))
            link(v.tensor_tensor(big3[1], big3[1], lower[:, :, :].unsqueeze(1).broadcast_to((P, NT, E, E)), ALU.mult))
            link(v.tensor_tensor(big3[0], big3[0], big3[1], ALU.add))
            link(v.tensor_reduce(rank, big3[0], AX_X, ALU.add))
            v.tensor_scalar(sel, rank, 2.0, None, ALU.is_lt).then_inc(sel_ready, 1)
            v.wait_ge(sel_ready, 1)
            v.wait_ge(gate_exp, 1)
            link(v.tensor_reduce(total, ex, AX_X, ALU.add))
            link(v.reciprocal(inv, total))
            link(v.tensor_tensor(w, ex, b16(inv), ALU.mult))
            link(v.tensor_tensor(w, w, sel, ALU.mult))
            link(v.tensor_reduce(total, w, AX_X, ALU.add))
            link(v.reciprocal(inv, total))
            link(v.tensor_tensor(w, w, b16(inv), ALU.mult))
            v.wait_ge(pos_psum, 1)
            link(v.tensor_copy(pos, ps[:, 0, 0:NT * E].rearrange("p (t e) -> p t e", t=NT)))
            link(v.tensor_scalar(keep, pos, float(CAP), None, ALU.is_lt))
            link(v.tensor_scalar(slot, pos, float(CAP - 1), None, ALU.min))
            link(v.tensor_tensor(slot, slot, first_slot[:, :].unsqueeze(1).broadcast_to((P, NT, E)), ALU.add))
            link(v.tensor_tensor(w, w, keep, ALU.mult))
            for k in range(2):
                link(v.tensor_scalar(pick, rank, float(k), None, ALU.is_equal))
                link(v.tensor_tensor(prod, pick, slot, ALU.mult))
                link(v.tensor_reduce(chosen, prod, AX_X, ALU.add))
                link(v.tensor_copy(idx_in[k], chosen))
                link(v.tensor_tensor(prod, pick, w, ALU.mult))
                link(v.tensor_reduce(weight[k], prod, AX_X, ALU.add))
                link(v.tensor_tensor(prod, pick, keep, ALU.mult))
                link(v.tensor_reduce(kept, prod, AX_X, ALU.add))
                link(v.tensor_scalar(kept, kept, -FAR, FAR, ALU.mult, ALU.add))
                link(v.tensor_tensor(chosen, chosen, kept, ALU.add))
                if k == 0:
                    link(v.tensor_copy(idx_out[k], chosen))
            v.tensor_copy(idx_out[1], chosen).then_inc(routed, 1)

            @peeled(v, E // 2)
            def _(pair):
                for i in range(2):
                    e = pair * 2 + i
                    v.tensor_copy(b1_e[i], b1T[:, bass.ds(e * NFE, NFE)]).then_inc(b1_ready, 1)
                    v.wait_ge(b2_in[i], pair * 16 + 16)
                    wait(v, eo_stored[i], pair * 32)
                    v.wait_ge(eo_psum, e + 1)
                    v.tensor_tensor(eout[i][:, 0:2, :], ps[:, 6, :].rearrange("p (j d) -> p j d", j=2),
                                    b2_row[i].unsqueeze(1).broadcast_to((P, 2, D)), ALU.add).then_inc(mix_step, 1)
                    v.tensor_tensor(eout[i][0:ROWS[2], 2, :], ps[0:ROWS[2], 7, 0:D], b2_row[i][0:ROWS[2], :], ALU.add)\
                        .then_inc(eo_out, 1)
            for t in range(NT):
                if t % GT == 0:
                    v.wait_ge(gathered[t // GT], 32 * GT)
                v.scalar_tensor_tensor(out=x2[:, t, :], in0=got[0][:, t, :], scalar=weight[0][:, t:t + 1],
                                       in1=x2[:, t, :], op0=ALU.mult, op1=ALU.add).then_inc(mix_step, 1)
                v.wait_ge(mix_step, 1 + E + t + 1)
                v.scalar_tensor_tensor(out=x2[:, t, :], in0=got[1][:, t, :], scalar=weight[1][:, t:t + 1],
                                       in1=x2[:, t, :], op0=ALU.mult, op1=ALU.add).then_inc(mixed, 1)

        @block.tensor
        def _(pe):
            pe.wait_ge(consts, 5)
            pe.wait_ge(gp_step, 8)
            pe.wait_ge(prep_dve, 1)
            pe.transpose(ps[:, 0, 0:NT], nm_f[:, :], ident[0:NT, 0:NT]).then_inc(prep_pe, 1)
            for k in range(ND):
                last = pe.transpose(ps[:, 1, k * E:(k + 1) * E], gw_rows[:, k * P:(k + 1) * P], ident[0:E, 0:E])
            last.then_inc(prep_pe, 1)
            pe.transpose(ps[:, 2, 0:E * NFE], b1_rows[:, :], ident[0:E * NFE, 0:E * NFE]).then_inc(prep_pe, 1)

            def turn_group(src, banks, done):
                for k in range(ND):
                    for j in range(GT):
                        last = pe.transpose(ps[:, banks + k, j * P:(j + 1) * P], src[:, j, k * P:(k + 1) * P], ident[:, :])
                last.then_inc(done, 1)

            pe.wait_ge(w_in, 16 * 4)
            pe.wait_ge(prep_dve, 5)
            @peeled(pe, NG)
            def _(g):
                pe.wait_ge(ht_ready, g + 1)
                wait(pe, v_out, 2 * g)
                turn_group(ht_c, 0, htT_psum)
                pe.wait_ge(hs_ready, g + 1)
                turn_group(hs_c, 2, hsT_psum)
                for w, src, bank, ready, done, out_sem in ((0, htT, 4, htT_out, q_psum, q_out),
                                                           (1, hsT, 6, hsT_out, k_psum, k_out)):
                    pe.wait_ge(ready, g + 1)
                    wait(pe, out_sem, ND * g)
                    for c in range(ND):
                        for k in range(ND):
                            last = pe.matmul(ps[:, bank + c, :], wqkvo[:, w, k, c * P:(c + 1) * P], src[:, k, :],
                                             start=(k == 0), stop=(k == ND - 1))
                    last.then_inc(done, 1)
                for j in range(GT):
                    for k in range(ND):
                        last = pe.matmul(ps[:, j // 2, (j % 2) * D:(j % 2 + 1) * D], hsT[:, k, j * P:(j + 1) * P],
                                         wqkvo[:, 2, k, :], start=(k == 0), stop=(k == ND - 1))
                    if j % 2:
                        last.then_inc(v_psum, 1)

            def score(it, k, half):
                n, s = it * UNITS + k, k % UNITS
                wait(pe, masked, 2 * (n - 1) + half + 1)
                at = (it * 2 + k // H) * P
                q = qst[:, s % H, bass.ds(at, P)] if not isinstance(at, int) else qst[:, s % H, at:at + P]
                for c in range(2):
                    last = pe.matmul(ps[:, 2 * half + c, :], q, kst[:, s % H, (2 * half + c) * 512:(2 * half + c + 1) * 512],
                                     start=True, stop=True)
                last.then_inc(scores, 1)

            def turn(it, k, g):
                n = it * UNITS + k
                if g == 0:
                    wait(pe, exp_done, n + 1)
                pk, pg = (k, g - 2) if g >= 2 else (k - 1, g + 2)
                if not (isinstance(n, int) and n == 0 and g < 2):
                    by = evacuated_by(pk, pg)
                    wait(pe, evac[by], evac_count(by, it, pk, pg))
                for b in range(4):
                    s = 4 * g + b
                    last = pe.transpose(ps[:, 4 + g % 2, b * P:(b + 1) * P], logits[k % RING][:, s * P:(s + 1) * P], ident[:, :])
                last.then_inc(turned, 1)

            def contexts(it, k, half):
                n, h = it * UNITS + k, k % H
                if half == 0:
                    for by in ("act", "dve"):
                        wait(pe, evac[by], evac_count(by, it, k, 3))
                    if k % HG == 0:
                        wait(pe, part_out, it * (UNITS // HG) + k // HG)
                for s in range(8 * half, 8 * half + 8):
                    j = s % 4
                    last = pe.matmul(ps[j * HD:(j + 1) * HD, 6, (h % HG) * P:(h % HG + 1) * P],
                                     vals[:, s, h * HD:(h + 1) * HD], probsT[k % 2][:, s * P:(s + 1) * P],
                                     start=(s < 4), stop=(s >= 12))
                if half:
                    last.then_inc(pv_done, 1)

            def fold_parts(it, k):
                G, g2 = it * (UNITS // HG) + (k - 6) // HG, ((k - 6) // HG) % 2
                wait(pe, part_out, G + 1)
                if g2 == 0:
                    wait(pe, ctx_ready, it * 2 + (k - 6) // H)
                for h in range(HG):
                    at = (g2 * HG + h) * HD
                    last = pe.matmul(ps[:, 7, at:at + HD], ctx_part[:, h * P:(h + 1) * P], fold[:, :],
                                     start=True, stop=True)
                last.then_inc(folded, 1)

            def pe_round(it, first, last):
                for k in range(UNITS):
                    turn(it, k, 0)
                    turn(it, k, 1)
                    if not (last and k + AHEAD_QK >= UNITS):
                        score(it, k + AHEAD_QK, 0)
                    if not (first and k == 0):
                        contexts(it, k - 1, 0)
                    turn(it, k, 2)
                    turn(it, k, 3)
                    if not (last and k + AHEAD_QK >= UNITS):
                        score(it, k + AHEAD_QK, 1)
                    if not (first and k == 0):
                        contexts(it, k - 1, 1)
                    if k % HG == 2 and not (first and k < 6):
                        fold_parts(it, k)

            pe.wait_ge(stacked, 16 * NG * 32)
            pe.wait_ge(v_out, 2 * NG)
            for k in range(AHEAD_QK):
                for half in range(2):
                    score(0, k, half)
            rounds(pe, pe_round)
            contexts(ROUNDS, -1, 0)
            contexts(ROUNDS, -1, 1)
            fold_parts(ROUNDS, 2)

            pe.wait_ge(w2_in, 32)
            @peeled(pe, NG)
            def _(c):
                pe.wait_ge(cx_copied, c + 1)
                turn_group(cx_c, 0, cxT_psum)
                pe.wait_ge(cxT_out, c + 1)
                wait(pe, gate_out, c)
                for j in range(GT):
                    for k in range(ND):
                        last = pe.matmul(ps[:, 2 + j // 2, (j % 2) * D:(j % 2 + 1) * D], ctxT[:, k, j * P:(j + 1) * P],
                                         wqkvo[:, 3, k, :], start=(k == 0), stop=(k == ND - 1))
                last.then_inc(wo_psum, 1)
                pe.wait_ge(u_ready, c + 1)
                turn_group(u_c, 0, uT_psum)
                pe.wait_ge(uT_out, c + 1)
                for f in range(NF):
                    wait(pe, h_out, c * NF + f - 3)
                    for k in range(ND):
                        last = pe.matmul(ps[:, 4 + f % 4, :], w1_sb[:, k, f * P:(f + 1) * P], uT[:, k, :],
                                         start=(k == 0), stop=(k == ND - 1))
                    last.then_inc(h_psum, 1)
                pe.wait_ge(h_out, c * NF + NF)
                for j in range(GT):
                    for f in range(NF):
                        last = pe.matmul(ps[:, 2 + j // 2, (j % 2) * D:(j % 2 + 1) * D], hid[:, f, j * P:(j + 1) * P],
                                         w2_sb[:, f, :], start=(f == 0), stop=(f == NF - 1))
                last.then_inc(y_psum, 1)
                pe.wait_ge(xn3_ready, c * GT + GT)
                turn_group(xn3_c, 0, n3T_psum)
                pe.wait_ge(n3T_out, c + 1)
                for j in range(GT):
                    for k in range(ND):
                        last = pe.matmul(ps[:, 2, j * E:(j + 1) * E], xn3T[:, k, j * P:(j + 1) * P], gwT[:, k, :],
                                         start=(k == 0), stop=(k == ND - 1))
                last.then_inc(gate_psum, 1)

            pe.wait_ge(sel_ready, 1)
            pe.matmul(ps[:, 0, 0:NT * E], before[:, :], small[4], start=True, stop=False)
            for t in range(1, NT):
                last = pe.matmul(ps[:, 0, t * E:NT * E].rearrange("p (t e) -> p t e", e=E), ones[:, :],
                                 small[4][:, t - 1:t, :].broadcast_to((P, NT - t, E)), start=False, stop=(t == NT - 1))
            last.then_inc(pos_psum, 1)

            pe.wait_ge(routed, 1)
            @peeled(pe, E // 2)
            def _(pair):
                for i in range(2):
                    e = pair * 2 + i
                    pe.wait_ge(xin_in[i], pair * 32 + 32)
                    for k in range(ND):
                        for j, r in enumerate(ROWS):
                            last = pe.transpose(ps[:, k, j * P:j * P + r], xin[i][0:r, j, k * P:(k + 1) * P], ident[0:r, 0:r])
                    last.then_inc(xinT_psum, 1)
                    pe.wait_ge(ew_in[i], pair * 32 + 32)
                    pe.wait_ge(xinT_out, e + 1)
                    for f in range(NFE):
                        wait(pe, eh_out, e * NFE + f - 3)
                        for k in range(ND):
                            last = pe.matmul(ps[:, 2 + f % 4, 0:CAP], ew1[i][:, k, f * P:(f + 1) * P], xinT[:, k, :],
                                             start=(k == 0), stop=(k == ND - 1))
                        last.then_inc(eh_psum, 1)
                    pe.wait_ge(eh_out, e * NFE + NFE)
                    wait(pe, eo_out, e)
                    for j, r in enumerate(ROWS):
                        dst = ps[:, 6, j * D:(j + 1) * D] if j < 2 else ps[0:r, 7, 0:D]
                        for f in range(NFE):
                            last = pe.matmul(dst, ehid[i][:, f, j * P:j * P + r], ew2[i][:, f, :],
                                             start=(f == 0), stop=(f == NFE - 1))
                    last.then_inc(eo_psum, 1)


_INS = ["x", "adj", "nodemask", "L0_gnn_h_target", "L0_gnn_ln1_scale", "L0_gnn_ln1_bias", "L0_gnn_Wq", "L0_gnn_bq",
        "L0_gnn_Wk", "L0_gnn_bk", "L0_gnn_Wv", "L0_gnn_bv", "L0_gnn_Wo", "L0_gnn_bo", "L0_gnn_ln2_scale",
        "L0_gnn_ln2_bias", "L0_gnn_W1", "L0_gnn_W2", "L0_ffn_gate_w", "L0_ffn_w1", "L0_ffn_b1", "L0_ffn_w2",
        "L0_ffn_b2"]


def kernel(**inputs):
    import numpy as np
    import concourse.bacc as bacc
    from concourse.bass_utils import run_bass_kernel_spmd as run

    nc = bacc.Bacc("TRN2", target_bir_lowering=False, num_devices=1)
    arrays, args = {}, []
    for name in _INS:
        a = np.ascontiguousarray(inputs[name])
        arrays[f"in_{name}"] = a
        args.append(nc.dram_tensor(f"in_{name}", a.shape, mybir.dt.from_np(a.dtype), kind="ExternalInput").ap())
    out = nc.dram_tensor("out", inputs["x"].shape, F32, kind="ExternalOutput").ap()
    build(nc, *args, out)
    r = run(nc, [arrays], core_ids=[0])
    return r.results[0]["out"]
```

```python
from contextlib import ExitStack

import concourse.bass as bass
import concourse.mybir as mybir

F32 = mybir.dt.float32
F16 = mybir.dt.float16
BF16 = mybir.dt.bfloat16
I32 = mybir.dt.int32
ALU = mybir.AluOpType
ACT = mybir.ActivationFunctionType
AX_X = mybir.AxisListType.X

P = 128
EPS = 1e-5
BIG = 1e30
AHEAD_QK = 3
RING = 4
UNITS = 16


def evacuated_by(k, g):
    return "act" if g in (0, 2) or (g == 1 and k % 4 == 0) else "dve"


def evac_count(engine, it, k, g):
    four = {"act": 9, "dve": 7}[engine]
    within = sum(evacuated_by(kk, gg) == engine
                 for kk in range(k % 4 + 1) for gg in range(4) if (kk, gg) <= (k % 4, g))
    return it * (four * UNITS // 4) + (k // 4) * four + within


def wait(eng, sem, value):
    if not isinstance(value, int) or value > 0:
        eng.wait_ge(sem, value)


def peeled(eng, n):
    def run(body):
        body(0)
        with eng.Fori(1, n) as i:
            body(i)
    return run


def hold(eng, sem, value, passed):
    wait(eng, sem, value)
    eng.sem_inc(passed, 1)


def build(nc, x, adj, nodemask, h_target, ln1_scale, ln1_bias, Wq, bq, Wk, bk, Wv, bv, Wo, bo,
          ln2_scale, ln2_bias, W1, W2, gate_w, w1, b1, w2, b2, out):
    N, D = x.shape
    H, HD = 8, D // 8
    NT = N // P
    ND = D // P
    F = W1.shape[1]
    NF = F // P
    E, NFE = w1.shape[0], w1.shape[2] // P
    CAP = -(-5 * N // (4 * E))
    SLOTS = E * CAP
    ROWS = [P, P, CAP - 2 * P]
    NG = 4
    GT = NT // NG
    GW = GT * P
    ROUNDS = NT * H // UNITS
    HG = 4
    SCALE = 1.0 / float(HD) ** 0.5
    FAR = float(1 << 20)
    assert GW == 512 and NT == 16 and 4 * HD == P and UNITS == 2 * H

    slots_in = nc.dram_tensor("slots_in", (SLOTS, D), F32, kind="Internal").ap()
    slots_out = nc.dram_tensor("slots_out", (SLOTS, D), F32, kind="Internal").ap()

    with ExitStack() as ctx:
        def sb(name, shape, dt=F32):
            return ctx.enter_context(nc.sbuf_tensor(name, shape, dt))

        def sem(name):
            return ctx.enter_context(nc.semaphore(name))

        ps = ctx.enter_context(nc.psum_tensor("ps", [P, 8, 512], F32))

        xn = sb("xn", [P, NT, D])
        ht = sb("ht", [P, NT, D])
        vals = sb("vals", [P, NT, D])
        keys_q_arena = sb("keys_q_arena", [P, 16384])
        work = sb("work", [P, 12800])
        wqkvo = sb("wqkvo", [P, 4, ND, D])
        w1_sb = sb("w1_sb", [P, ND, F])
        adj_sb = sb("adj_sb", [P, N], I32)
        mask_sb = [sb(f"mask{i}", [P, N], BF16) for i in range(2)]
        rows_sb = sb("rows_sb", [P, 6, D])
        ident = sb("ident", [P, P])
        fold = sb("fold", [P, HD])
        before = sb("before", [P, P])
        ones = sb("ones", [P, P])
        lower = sb("lower", [P, E, E])
        first_slot = sb("first_slot", [P, E])
        choice = sb("choice", [P, 2, E])
        cols = sb("cols", [P, 4, ND])
        nm_i = sb("nm_i", [NT, P], I32)
        nm_f = sb("nm_f", [NT, P])
        nmask = sb("nmask", [P, NT])
        gw_rows = sb("gw_rows", [E, D])
        gwT = sb("gwT", [P, ND, E])
        b1_rows = sb("b1_rows", [E * NFE, P])
        b1T = sb("b1T", [P, E * NFE])
        stats = sb("stats", [P, 2 * NT, 6])
        mean = sb("mean", [P, 2 * NT])
        tmpa = sb("tmpa", [P, 2 * NT])
        tmpb = sb("tmpb", [P, 2 * NT])
        vare = sb("vare", [P, 2 * NT])
        sdev = sb("sdev", [P, 2 * NT])
        rstd = sb("rstd", [P, 2 * NT])
        least = sb("least", [P, 2, UNITS])
        rowsum = sb("rowsum", [P, 2, UNITS])
        rows2 = sb("rows2", [P, 2, H])
        rinv = sb("rinv", [P, 2, H])

        def view(arena, at, words, dt=F32):
            a = arena[:, at:at + words]
            return a if dt == F32 else a.bitcast(dt)

        kst = view(keys_q_arena, 0, 8192, F16).rearrange("p (h n) -> p h n", h=H)
        qst = view(keys_q_arena, 8192, 8192, F16).rearrange("p (h n) -> p h n", h=H)
        hsT = view(work, 0, 1024).rearrange("p (k n) -> p k n", k=ND)
        htT = view(work, 1024, 1024).rearrange("p (k n) -> p k n", k=ND)
        q_f = view(work, 2048, 1024).rearrange("p (k n) -> p k n", k=ND)
        k_f = view(work, 3072, 1024).rearrange("p (k n) -> p k n", k=ND)
        split = [view(work, 4096 + 2048 * i, 2048, F16).rearrange("p (k n) -> p k n", k=ND)
                 for i in range(4)]
        logits = [view(work, 2048 * i, 2048) for i in range(RING)]
        probsT = [view(work, 8192 + 2048 * i, 2048) for i in range(2)]
        ctx_part = view(work, 12288, 512)
        hs_c, ht_c = w1_sb[:, 0, :].rearrange("p (j d) -> p j d", j=GT), w1_sb[:, 1, :].rearrange("p (j d) -> p j d", j=GT)

        x2 = view(keys_q_arena, 0, 4096).rearrange("p (t d) -> p t d", t=NT)
        w2_sb = view(keys_q_arena, 4096, 2048).rearrange("p (k d) -> p k d", k=NF)
        ctxT = view(keys_q_arena, 6144, 1024).rearrange("p (k n) -> p k n", k=ND)
        hid = view(keys_q_arena, 7168, 4096).rearrange("p (f n) -> p f n", f=NF)
        u_c = view(keys_q_arena, 11264, 1024).rearrange("p (j d) -> p j d", j=GT)
        uT = view(keys_q_arena, 12288, 1024).rearrange("p (k n) -> p k n", k=ND)
        xn3T = view(keys_q_arena, 13312, 1024).rearrange("p (k n) -> p k n", k=ND)
        gates, rank, sel, pos, z, ex, w, keep = (view(work, NT * E * i, NT * E).rearrange("p (t e) -> p t e", t=NT)
                                                 for i in range(8))
        larger, same = (view(work, 1024 + 256 * i, 256).rearrange("p (t a b) -> p t a b", t=GT, a=E) for i in range(2))
        pick, prod_in, prod_out = (view(work, 1536 + 64 * i, 64).rearrange("p (t k e) -> p t k e", t=GT, k=2)
                                   for i in range(3))
        from_slot, to_slot, over = (view(work, 1728 + 32 * i, 32).rearrange("p (t e) -> p t e", t=GT) for i in range(3))
        chosen_in, chosen_out = (view(work, 1824 + 8 * i, 8).rearrange("p (t k) -> p t k", t=GT) for i in range(2))
        chunk_sel, sel_before = (view(work, 1840 + 8 * i, 8) for i in range(2))
        top, total, inv = (view(work, 1856 + 16 * i, 16) for i in range(3))
        weight = [view(work, 1904 + 16 * i, 16) for i in range(2)]
        idx_in, idx_out = (view(work, 1936 + 32 * i, 32, I32).rearrange("p (t k) -> p t k", t=NT) for i in range(2))
        xin = [view(work, 2048 + 768 * i, 768).rearrange("p (j d) -> p j d", j=3) for i in range(2)]
        b2_row = [view(work, 3584 + 256 * i, 256) for i in range(2)]
        ew1 = [view(work, 4096 + 2048 * i, 2048).rearrange("p (k f) -> p k f", k=ND) for i in range(2)]
        ew2 = [view(work, 8192 + 2048 * i, 2048).rearrange("p (k d) -> p k d", k=NFE) for i in range(2)]
        b1_e = [view(work, 12288 + 8 * i, 8) for i in range(2)]
        xinT = view(keys_q_arena, 4096, 640).rearrange("p (k n) -> p k n", k=ND)
        ehid = [view(keys_q_arena, 4736 + 2560 * i, 2560).rearrange("p (f n) -> p f n", f=NFE)
                for i in range(2)]
        eout = [view(keys_q_arena, 9856 + 768 * i, 768).rearrange("p (j d) -> p j d", j=3) for i in range(2)]
        got = [xn, ht]

        x_in = [sem(f"x_in{g}") for g in range(NG)]
        ht_in = [sem(f"ht_in{g}") for g in range(NG)]
        w_in, small_in, zero_done = map(sem, ("w_in", "small_in", "zero_done"))
        consts, gp_step, zeros_set = map(sem, ("consts", "gp_step", "zeros_set"))
        ln_step, sqrt_done = sem("ln_step"), sem("sqrt_done")
        prep_dve, prep_pe = sem("prep_dve"), sem("prep_pe")
        x_scaled, norm_x_step = sem("x_scaled"), sem("norm_x_step")
        hs_ready, ht_ready, norm_t_step = sem("hs_ready"), sem("ht_ready"), sem("norm_t_step")
        htT_psum, hsT_psum, htT_out, hsT_out = map(sem, ("htT_psum", "hsT_psum", "htT_out", "hsT_out"))
        q_psum, k_psum, v_psum, q_out, k_out, v_out = map(
            sem, ("q_psum", "k_psum", "v_psum", "q_out", "k_out", "v_out"))
        split_step, split_done = sem("split_step"), sem("split_done")
        stacked = [sem(f"stacked{hq}") for hq in range(4)]
        adj_in, mask_ready, mask_used = sem("adj_in"), sem("mask_ready"), sem("mask_used")
        scores, masked = sem("scores"), sem("masked")
        exp_done, turned = sem("exp_done"), sem("turned")
        pool_passed, dve_passed = sem("pool_passed"), sem("dve_passed")
        evac = {"act": sem("evac_act"), "dve": sem("evac_dve")}
        pv_done, part_out, folded = sem("pv_done"), sem("part_out"), sem("folded")
        rinv_done, ctx_ready = sem("rinv_done"), sem("ctx_ready")
        w1_in, w2_in, x2_in = sem("w1_in"), sem("w2_in"), sem("x2_in")
        cxT_psum, cxT_out, wo_psum, attn_step, u_ready = map(
            sem, ("cxT_psum", "cxT_out", "wo_psum", "attn_step", "u_ready"))
        uT_psum, uT_out, h_psum, h_out, y_psum, y_out, xn3_ready = map(
            sem, ("uT_psum", "uT_out", "h_psum", "h_out", "y_psum", "y_out", "xn3_ready"))
        n3T_psum, n3T_out, gate_psum, gate_out = map(sem, ("n3T_psum", "n3T_out", "gate_psum", "gate_out"))
        ln2_step, ln3_step, sqrt2, sqrt3 = map(sem, ("ln2_step", "ln3_step", "sqrt2", "sqrt3"))
        rank_step, sel_ready, pos_psum, pos_out, slot_step = map(
            sem, ("rank_step", "sel_ready", "pos_psum", "pos_out", "slot_step"))
        weight_step, gate_exp = sem("weight_step"), sem("gate_exp")
        routed, scattered = sem("routed"), sem("scattered")
        ew_in, xin_in, b2_in, eo_stored = ([sem(f"{name}{i}") for i in range(2)]
                                           for name in ("ew_in", "xin_in", "b2_in", "eo_stored"))
        xinT_psum, xinT_out, eh_psum, eh_out, eo_psum, eo_out, b1_ready = map(
            sem, ("xinT_psum", "xinT_out", "eh_psum", "eh_out", "eo_psum", "eo_out", "b1_ready"))
        gathered = [sem(f"gathered{g}") for g in range(NG)]
        mixed, mix_step, stored = sem("mixed"), sem("mix_step"), sem("stored")

        def moments(v, n, st, base, ln_step=ln_step):
            m, a, b, ve, r = mean[:, 0:n], tmpa[:, 0:n], tmpb[:, 0:n], vare[:, 0:n], rstd[:, 0:n]
            v.tensor_tensor(m, st[:, :, 1], st[:, :, 4], ALU.add).then_inc(ln_step, 1)
            v.tensor_tensor(a, st[:, :, 1], st[:, :, 4], ALU.subtract).then_inc(ln_step, 1)
            v.tensor_tensor(b, st[:, :, 2], st[:, :, 5], ALU.add).then_inc(ln_step, 1)
            v.wait_ge(ln_step, base + 3)
            v.tensor_scalar(m, m, 0.5, None, ALU.mult).then_inc(ln_step, 1)
            v.scalar_tensor_tensor(out=ve, in0=a, scalar=0.25, in1=a, op0=ALU.mult, op1=ALU.mult).then_inc(ln_step, 1)
            v.wait_ge(ln_step, base + 5)
            v.scalar_tensor_tensor(out=a, in0=b, scalar=1.0 / D, in1=ve, op0=ALU.mult, op1=ALU.add).then_inc(ln_step, 1)
            v.wait_ge(ln_step, base + 6)
            v.tensor_scalar(ve, a, EPS, None, ALU.add).then_inc(ln_step, 1)

        def inverse_root(v, n, base, root_sem, root_count, ln_step=ln_step):
            a, ve, r = tmpa[:, 0:n], vare[:, 0:n], rstd[:, 0:n]
            v.wait_ge(root_sem, root_count)
            v.reciprocal(r, sdev[:, 0:n]).then_inc(ln_step, 1)
            v.wait_ge(ln_step, base + 8)
            v.tensor_tensor(a, r, r, ALU.mult).then_inc(ln_step, 1)
            v.wait_ge(ln_step, base + 9)
            v.tensor_tensor(a, a, ve, ALU.mult).then_inc(ln_step, 1)
            v.wait_ge(ln_step, base + 10)
            v.tensor_scalar(a, a, -0.5, 1.5, ALU.mult, ALU.add).then_inc(ln_step, 1)
            v.wait_ge(ln_step, base + 11)
            v.tensor_tensor(r, r, a, ALU.mult).then_inc(ln_step, 1)
            v.wait_ge(ln_step, base + 12)

        LN_STEPS = 12
        LN_CHUNK = GT + LN_STEPS
        A_STEPS = 10
        RANK_STEPS, SLOT_STEPS = 5, 13

        def rounds(eng, body):
            body(0, True, False)
            with eng.Fori(1, ROUNDS - 1) as it:
                body(it, False, False)
            body(ROUNDS - 1, False, True)

        block = ctx.enter_context(nc.Block())

        @block.sync
        def _(sp):
            for dst, src, s in ((ht, h_target, ht_in), (xn, x, x_in)):
                for g in range(NG):
                    sp.dma_start(dst[:, g * GT:(g + 1) * GT, :],
                                 src[g * GW:(g + 1) * GW, :].rearrange("(j p) d -> p j d", p=P)).then_inc(s[g], 16)
            sp.dma_start(nm_i[:, :], nodemask.rearrange("(t p) -> t p", p=P)).then_inc(small_in, 16)
            sp.dma_start(gw_rows[:, :], gate_w[:, :]).then_inc(small_in, 16)
            sp.dma_start(b1_rows[:, :], b1.rearrange("e (f p) -> (e f) p", p=P)).then_inc(small_in, 16)
            for i, r in enumerate((bq, bk)):
                sp.dma_start(cols[:, i, :], r.rearrange("(c p) -> p c", p=P), allow_slow_non_contiguous=True).then_inc(small_in, 16)
            for i, r in enumerate((ln1_scale, ln1_bias, bv, bo, ln2_scale, ln2_bias)):
                sp.dma_start(rows_sb[:, i, :], r.partition_broadcast(P)).then_inc(small_in, 16)
            for i, w in enumerate((Wq, Wk, Wv, Wo)):
                sp.dma_start(wqkvo[:, i, :, :], w.rearrange("(k p) n -> p k n", p=P)).then_inc(w_in, 16)
            sp.dma_start(adj_sb[:, :], adj[0:P, :]).then_inc(adj_in, 16)
            sp.wait_ge(zeros_set, 1)
            zeros = slots_in.rearrange("(p r) d -> p (r d)", p=P)
            for at in range(0, SLOTS * D // P, N // 2):
                sp.dma_start(zeros[:, at:at + N // 2], mask_sb[1][:, :].bitcast(F32)).then_inc(zero_done, 16)
            sp.wait_ge(mask_ready, 1)
            sp.dma_start(adj_sb[:, :], adj[P:2 * P, :]).then_inc(adj_in, 16)

            with sp.Fori(0, NG) as g:
                sp.wait_ge(split_done, 2 * g + 2)
                for hq in range(4):
                    for dst, parts in ((qst, (0, 0, 1, 1)), (kst, (2, 3, 2, 3))):
                        for slot, part in enumerate(parts):
                            sp.dma_start(
                                dst[HD * slot:HD * (slot + 1), hq:H:4, bass.ds(g * GW, GW)],
                                split[part][HD * hq:HD * (hq + 1), :, bass.ds(g * GW, GW)]).then_inc(stacked[hq], 16)

            sp.wait_ge(htT_psum, NG)
            sp.wait_ge(hsT_psum, NG)
            sp.dma_start(w1_sb[:, :, :], W1.rearrange("(k p) n -> p k n", p=P)).then_inc(w1_in, 16)
            with sp.Fori(2, NT) as t:
                sp.wait_ge(mask_ready, t)
                sp.dma_start(adj_sb[:, :], adj[bass.ds(t * P, P), :]).then_inc(adj_in, 16)

            sp.wait_ge(ctx_ready, NT)
            sp.dma_start(x2[:, :, :], x.rearrange("(t p) d -> p t d", p=P)).then_inc(x2_in, 16)
            sp.dma_start(w2_sb[:, :, :], W2.rearrange("(k p) n -> p k n", p=P)).then_inc(w2_in, 16)

            def load_weights(e, i):
                sp.dma_start(ew1[i], w1[bass.ds(e, 1), :, :].rearrange("e (k p) f -> p (e k) f", p=P)).then_inc(ew_in[i], 16)
                sp.dma_start(ew2[i], w2[bass.ds(e, 1), :, :].rearrange("e (k p) f -> p (e k) f", p=P)).then_inc(ew_in[i], 16)
                sp.dma_start(b2_row[i], b2[bass.ds(e, 1), :].rearrange("e d -> (e d)").partition_broadcast(P)).then_inc(b2_in[i], 16)

            def load_rows(e, i):
                sp.dma_start(xin[i][:, 0:2, :],
                             slots_in[bass.ds(e * CAP, 2 * P), :].rearrange("(j p) d -> p j d", p=P)).then_inc(xin_in[i], 16)
                sp.dma_start(xin[i][0:ROWS[2], 2, :],
                             slots_in[bass.ds(e * CAP + 2 * P, ROWS[2]), :]).then_inc(xin_in[i], 16)

            load_weights(0, 0)
            load_weights(1, 1)
            sp.wait_ge(scattered, 16 * 2 * NT)
            load_rows(0, 0)
            load_rows(1, 1)
            with sp.Fori(1, E // 2) as pair:
                for i in range(2):
                    sp.wait_ge(eo_out, 4 * pair + 2 * i - 2)
                    load_weights(pair * 2 + i, i)
                    load_rows(pair * 2 + i, i)

            with sp.Fori(0, NG) as g:
                sp.wait_ge(mixed, GT * g + GT)
                sp.dma_start(out[bass.ds(g * GW, GW), :].rearrange("(j p) d -> p j d", p=P),
                             x2[:, bass.ds(g * GT, GT), :]).then_inc(stored, 16)
            sp.wait_ge(stored, 16 * NG)

        @block.gpsimd
        def _(pool):
            pool.memset(mask_sb[1][:, :], 0.0).then_inc(zeros_set, 1)
            for k in range(2):
                pool.memset(choice[:, k, :], float(k)).then_inc(consts, 1)
            pool.memset(ident[:, :], 0.0).then_inc(gp_step, 1)
            pool.memset(fold[:, :], 0.0).then_inc(gp_step, 1)
            pool.memset(before[:, :], 1.0).then_inc(gp_step, 1)
            pool.memset(lower[:, :, :], 1.0).then_inc(gp_step, 1)
            pool.memset(ones[:, :], 1.0).then_inc(consts, 1)
            pool.iota(first_slot[:, :], [[CAP, E]], base=0, channel_multiplier=0,
                      allow_small_or_imprecise_dtypes=True).then_inc(consts, 1)
            pool.wait_ge(gp_step, 4)
            pool.affine_select(out=ident[:, :], in_=ident[:, :], compare_op=ALU.not_equal, fill=1.0,
                               base=0, pattern=[[-1, P]], channel_multiplier=1).then_inc(consts, 1)
            pool.affine_select(out=before[:, :], in_=before[:, :], compare_op=ALU.is_gt, fill=0.0,
                               base=0, pattern=[[1, P]], channel_multiplier=-1).then_inc(consts, 1)
            pool.affine_select(out=lower[:, :, :], in_=lower[:, :, :], compare_op=ALU.is_gt, fill=0.0,
                               base=0, pattern=[[1, E], [-1, E]], channel_multiplier=0).then_inc(consts, 1)
            for j in range(P // HD):
                pool.affine_select(out=fold[:, :], in_=fold[:, :], compare_op=ALU.not_equal, fill=1.0,
                                   base=-HD * j, pattern=[[-1, HD]], channel_multiplier=1).then_inc(gp_step, 1)
                pool.wait_ge(gp_step, 5 + j)
            for m in range(2):
                if m:
                    pool.wait_ge(zero_done, 16 * (SLOTS * D // P // (N // 2)))
                pool.wait_ge(adj_in, 16 * (m + 1))
                pool.tensor_scalar(mask_sb[m][:, :], adj_sb[:, :], 0.0, BIG, ALU.is_equal, ALU.mult).then_inc(mask_ready, 1)
            pool.wait_ge(small_in, 16 * 11)
            pool.wait_ge(prep_dve, 3)
            @peeled(pool, NG)
            def _(g):
                hold(pool, x_scaled, GT * g + GT, pool_passed)
                src = xn[:, bass.ds(g * GT, GT), :]
                pool.tensor_tensor(src, src, rows_sb[:, 0, :].unsqueeze(1).broadcast_to((P, GT, D)), ALU.mult)\
                    .then_inc(norm_x_step, 1)
                hold(pool, norm_x_step, 2 * g + 1, pool_passed)
                pool.tensor_tensor(src, src, rows_sb[:, 1, :].unsqueeze(1).broadcast_to((P, GT, D)), ALU.add)\
                    .then_inc(norm_x_step, 1)
                pool.wait_ge(norm_x_step, 2 * g + 2)
                hold(pool, hsT_psum, g, pool_passed)
                pool.tensor_tensor(hs_c[:, :, :], src,
                                   nmask[:, bass.ds(g * GT, GT)].unsqueeze(2).broadcast_to((P, GT, D)), ALU.mult)\
                    .then_inc(hs_ready, 1)
            with pool.Fori(1, NT // 2) as pair:
                for m in range(2):
                    pool.wait_ge(adj_in, 32 * pair + 16 * m + 16)
                    hold(pool, mask_used, 2 * pair + m - 1, pool_passed)
                    pool.tensor_scalar(mask_sb[m][:, :], adj_sb[:, :], 0.0, BIG, ALU.is_equal, ALU.mult)\
                        .then_inc(mask_ready, 1)
            for t in range(NT):
                if t % GT == 0:
                    pool.wait_ge(routed, t // GT + 1)
                    if t == 0:
                        pool.wait_ge(zero_done, 16 * (SLOTS * D // P // (N // 2)))
                for k in range(2):
                    pool.indirect_dma_start(out=slots_in, out_offset=bass.IndirectOffsetOnAxis(idx_out[:, t, k:k + 1], 0),
                                            in_=vals[:, t, :], in_offset=None, bounds_check=SLOTS - 1,
                                            oob_is_err=False).then_inc(scattered, 16)
            for i in range(2):
                pool.wait_ge(eo_stored[i], 32 * E // 2)
            for t in range(NT):
                for k in range(2):
                    pool.indirect_dma_start(out=got[k][:, t, :], out_offset=None, in_=slots_out,
                                            in_offset=bass.IndirectOffsetOnAxis(idx_in[:, t, k:k + 1], 0))\
                        .then_inc(gathered[t // GT], 16)

        @block.scalar
        def _(act):
            act.wait_ge(ln_step, 32 + 7)
            act.activation(sdev[:, 0:2 * NT], vare[:, 0:2 * NT], ACT.Sqrt).then_inc(sqrt_done, 1)
            act.wait_ge(ln_step, 32 + LN_STEPS + 16 + 7)
            act.activation(sdev[:, 0:NT], vare[:, 0:NT], ACT.Sqrt).then_inc(sqrt_done, 1)
            act.wait_ge(prep_dve, 6)
            with act.Fori(0, NG) as g:
                act.wait_ge(htT_psum, g + 1)
                act.activation(htT[:, :, :], ps[:, 0:2, :], ACT.Copy).then_inc(htT_out, 1)
                act.wait_ge(hsT_psum, g + 1)
                act.activation(hsT[:, :, :], ps[:, 2:4, :], ACT.Copy).then_inc(hsT_out, 1)
                act.wait_ge(q_psum, g + 1)
                for c in range(ND):
                    act.activation(q_f[:, c, :], ps[:, 4 + c, :], ACT.Identity, bias=cols[:, 2, c:c + 1],
                                   scale=-SCALE).then_inc(q_out, 1)
                act.wait_ge(k_psum, g + 1)
                for c in range(ND):
                    act.activation(k_f[:, c, :], ps[:, 6 + c, :], ACT.Identity, bias=cols[:, 1, c:c + 1])\
                        .then_inc(k_out, 1)

            def exponentials(it, k, half):
                n, s = it * UNITS + k, k % UNITS
                if half == 0:
                    wait(act, masked, 2 * n + 2)
                    if s % H == 0:
                        wait(act, ctx_ready, it * 2 + k // H - 1)
                part = logits[s % RING][:, half * 1024:(half + 1) * 1024]
                act.activation(part, part, ACT.Exp, bias=least[:, 1, s:s + 1], scale=-1.0,
                               accum_out=rowsum[:, half, s:s + 1]).then_inc(exp_done, 1)

            def copy_out(it, k, g):
                n = it * UNITS + k
                if g == 0:
                    wait(act, pv_done, n - 1)
                wait(act, turned, 4 * n + g + 1)
                act.activation(probsT[k % 2][:, g * 512:(g + 1) * 512], ps[:, 4 + g % 2, :], ACT.Copy)\
                   .then_inc(evac["act"], 1)

            def partial_contexts(it, k):
                G = it * (UNITS // HG) + (k - 5) // HG
                wait(act, pv_done, G * HG + HG)
                wait(act, folded, G)
                act.activation(ctx_part, ps[:, 6, :], ACT.Copy).then_inc(part_out, 1)

            def act_round(it, first, last):
                for k in range(UNITS):
                    if k % HG == 1 and not (first and k < 5):
                        partial_contexts(it, k)
                    for g in range(4):
                        if evacuated_by(k, g) == "act":
                            copy_out(it, k, g)
                        if g % 2 == 1 and not (last and k + 2 >= UNITS):
                            exponentials(it, k + 2, g // 2)

            for k in range(2):
                for half in range(2):
                    exponentials(0, k, half)
            for hq in range(4):
                act.wait_ge(stacked[hq], 16 * NG * 8)
            rounds(act, act_round)
            partial_contexts(ROUNDS, 1)

            def turned_contexts(c):
                act.wait_ge(cxT_psum, c + 1)
                act.activation(ctxT[:, :, :], ps[:, 0:2, :], ACT.Copy).then_inc(cxT_out, 1)

            def root_of_norm(c, ln_step, root):
                act.wait_ge(ln_step, c * LN_CHUNK + GT + 7)
                act.activation(sdev[:, 0:GT], vare[:, 0:GT], ACT.Sqrt).then_inc(root, 1)

            def turned_norm3(c):
                act.wait_ge(n3T_psum, c + 1)
                act.activation(xn3T[:, :, :], ps[:, 0:2, :], ACT.Copy).then_inc(n3T_out, 1)

            turned_contexts(0)
            root_of_norm(0, ln2_step, sqrt2)
            for c in range(NG):
                act.wait_ge(uT_psum, c + 1)
                act.activation(uT[:, :, :], ps[:, 0:2, :], ACT.Copy).then_inc(uT_out, 1)
                for f in range(NF):
                    act.wait_ge(h_psum, c * NF + f + 1)
                    act.activation(hid[:, f, :], ps[:, 4 + (f + 2) % 4, :], ACT.Gelu_apprx_tanh).then_inc(h_out, 1)
                    if f == 1 and c:
                        root_of_norm(c - 1, ln3_step, sqrt3)
                    if f == 3 and c < NG - 1:
                        turned_contexts(c + 1)
                if c:
                    turned_norm3(c - 1)
                if c < NG - 1:
                    root_of_norm(c + 1, ln2_step, sqrt2)
            root_of_norm(NG - 1, ln3_step, sqrt3)
            turned_norm3(NG - 1)

            act.wait_ge(weight_step, 2)
            act.activation(ex, z, ACT.Exp).then_inc(gate_exp, 1)

            with act.Fori(0, E // 2) as pair:
                for i in range(2):
                    act.wait_ge(xinT_psum, pair * 2 + i + 1)
                    act.activation(xinT[:, :, :], ps[:, 0:2, 0:CAP], ACT.Copy).then_inc(xinT_out, 1)
                    act.wait_ge(b1_ready, pair * 2 + i + 1)
                    for f in range(NFE):
                        act.wait_ge(eh_psum, (pair * 2 + i) * NFE + f + 1)
                        act.activation(ehid[i][:, f, :], ps[:, 2 + f % 4, 0:CAP], ACT.Gelu,
                                       bias=b1_e[i][:, f:f + 1]).then_inc(eh_out, 1)
                    act.wait_ge(eo_out, 2 * (pair * 2 + i + 1))
                    act.dma_start(slots_out[bass.ds((pair * 2 + i) * CAP, 2 * P), :].rearrange("(j p) d -> p j d", p=P),
                                  eout[i][:, 0:2, :]).then_inc(eo_stored[i], 16)
                    act.dma_start(slots_out[bass.ds((pair * 2 + i) * CAP + 2 * P, ROWS[2]), :],
                                  eout[i][0:ROWS[2], 2, :]).then_inc(eo_stored[i], 16)

        @block.vector
        def _(v):
            for first, rows_in, arrived in ((0, ht, ht_in), (NT, xn, x_in)):
                for t in range(NT):
                    if t % GT == 0:
                        v.wait_ge(arrived[t // GT], 16)
                    v.bn_stats(stats[:, first + t, :], rows_in[:, t, :]).then_inc(ln_step, 1)
            v.wait_ge(ln_step, 32)
            moments(v, 2 * NT, stats, 32)
            v.wait_ge(small_in, 16 * 11)
            v.tensor_scalar(nm_f[:, :], nm_i[:, :], 1.0, None, ALU.is_equal).then_inc(prep_dve, 1)
            v.tensor_scalar(cols[:, 2, :], cols[:, 0, :], -SCALE, None, ALU.mult).then_inc(prep_dve, 1)
            v.wait_ge(prep_pe, 1)
            v.tensor_copy(nmask[:, :], ps[:, 0, 0:NT]).then_inc(prep_dve, 1)
            v.wait_ge(prep_pe, 2)
            v.tensor_copy(gwT[:, :, :], ps[:, 1, 0:ND * E].rearrange("p (k e) -> p k e", k=ND)).then_inc(prep_dve, 1)
            v.wait_ge(prep_pe, 3)
            v.tensor_copy(b1T[:, :], ps[:, 2, 0:E * NFE]).then_inc(prep_dve, 1)
            inverse_root(v, 2 * NT, 32, sqrt_done, 1)
            v.tensor_copy(tmpb[:, 0:1], rstd[:, 0:1]).then_inc(prep_dve, 1)
            with v.Fori(0, NG) as g:
                for j in range(GT):
                    t = xn[:, bass.ds(g * GT + j, 1), :]
                    v.tensor_scalar(t, t, mean[:, bass.ds(NT + g * GT + j, 1)], rstd[:, bass.ds(NT + g * GT + j, 1)],
                                    ALU.subtract, ALU.mult).then_inc(norm_t_step, 1)
                hold(v, norm_t_step, GT * g + GT, dve_passed)
                for j in range(GT):
                    v.bn_stats(stats[:, bass.ds(NT + g * GT + j, 1), :], xn[:, bass.ds(g * GT + j, 1), :]).then_inc(ln_step, 1)
            with v.Fori(0, NG) as g:
                for j in range(GT):
                    t = ht[:, bass.ds(g * GT + j, 1), :]
                    v.tensor_scalar(t, t, mean[:, bass.ds(g * GT + j, 1)], rstd[:, bass.ds(g * GT + j, 1)],
                                    ALU.subtract, ALU.mult).then_inc(norm_t_step, 1)
            v.wait_ge(norm_t_step, 2 * NT)
            v.wait_ge(ln_step, 32 + LN_STEPS + 16)
            moments(v, NT, stats[:, NT:2 * NT, :], 32 + LN_STEPS + 16)
            inverse_root(v, NT, 32 + LN_STEPS + 16, sqrt_done, 2)
            with v.Fori(0, NG) as g:
                for j in range(GT):
                    t = xn[:, bass.ds(g * GT + j, 1), :]
                    v.tensor_scalar(t, t, mean[:, bass.ds(g * GT + j, 1)], rstd[:, bass.ds(g * GT + j, 1)],
                                    ALU.subtract, ALU.mult).then_inc(x_scaled, 1)
            T0 = 2 * NT
            @peeled(v, NG)
            def _(g):
                t = ht[:, bass.ds(g * GT, GT), :]
                v.tensor_tensor(t, t, rows_sb[:, 0, :].unsqueeze(1).broadcast_to((P, GT, D)), ALU.mult).then_inc(norm_t_step, 1)
                v.wait_ge(norm_t_step, T0 + 3 * g + 1)
                v.tensor_tensor(t, t, rows_sb[:, 1, :].unsqueeze(1).broadcast_to((P, GT, D)), ALU.add).then_inc(norm_t_step, 1)
                v.wait_ge(norm_t_step, T0 + 3 * g + 2)
                v.tensor_tensor(t, t, nmask[:, bass.ds(g * GT, GT)].unsqueeze(2).broadcast_to((P, GT, D)), ALU.mult)\
                    .then_inc(norm_t_step, 1)
                v.wait_ge(norm_t_step, T0 + 3 * g + 3)
                hold(v, htT_psum, g, dve_passed)
                v.tensor_copy(ht_c[:, :, :], t).then_inc(ht_ready, 1)
                for src, hi, lo, done in ((q_f, split[0], split[1], q_out), (k_f, split[2], split[3], k_out)):
                    hold(v, done, ND * g + ND, dve_passed)
                    hi_g, lo_g = hi[:, :, bass.ds(g * GW, GW)], lo[:, :, bass.ds(g * GW, GW)]
                    v.tensor_copy(hi_g, src[:, :, :]).then_inc(split_step, 1)
                    v.wait_ge(split_step, 2 * g + (1 if done is q_out else 2))
                    v.tensor_tensor(lo_g, src[:, :, :], hi_g, ALU.subtract).then_inc(split_done, 1)
                for j in range(2):
                    v.wait_ge(v_psum, 2 * g + j + 1)
                    v.tensor_tensor(vals[:, bass.ds(g * GT + 2 * j, 2), :],
                                    ps[:, j, :].rearrange("p (j d) -> p j d", j=2),
                                    rows_sb[:, 2, :].unsqueeze(1).broadcast_to((P, 2, D)), ALU.add).then_inc(v_out, 1)

            def mask_and_reduce(it, k, half):
                n, s = it * UNITS + k, k % UNITS
                if half == 0:
                    wait(v, turned, 4 * (n - RING) + 4)
                    if s % H == 0:
                        wait(v, mask_ready, it * 2 + k // H + 1)
                else:
                    wait(v, masked, 2 * n + 1)
                hold(v, scores, 2 * n + half + 1, dve_passed)
                view3 = (lambda a: a[:, half * 1024:(half + 1) * 1024].rearrange("p (b n) -> p b n", b=2))
                v.tensor_tensor_reduce(
                    out=view3(logits[s % RING]), in0=ps[:, 2 * half:2 * half + 2, :],
                    in1=view3(mask_sb[s // H]), scale=1.0, scalar=3.0e38 if half == 0 else least[:, 0, s:s + 1],
                    op0=ALU.add, op1=ALU.min, accum_out=least[:, half, s:s + 1]).then_inc(masked, 1)

            def copy_out(it, k, g):
                n = it * UNITS + k
                wait(v, pv_done, n - 1)
                wait(v, turned, 4 * n + g + 1)
                v.tensor_copy(probsT[k % 2][:, g * 512:(g + 1) * 512], ps[:, 4 + g % 2, :]).then_inc(evac["dve"], 1)

            def normalise(it, k):
                t, par = it * 2 + (k - 11) // H, ((k - 11) // H) % 2
                wait(v, folded, 2 * t + 2)
                wait(v, exp_done, 2 * (8 * t + 8))
                v.tensor_tensor(rows2[:, par, :], rowsum[:, 0, par * H:par * H + H],
                                rowsum[:, 1, par * H:par * H + H], ALU.add).then_inc(rinv_done, 1)
                wait(v, rinv_done, 2 * t + 1)
                v.reciprocal(rinv[:, par, :], rows2[:, par, :]).then_inc(rinv_done, 1)
                wait(v, rinv_done, 2 * t + 2)
                dst = xn[:, bass.ds(t, 1), :] if not isinstance(t, int) else xn[:, t:t + 1, :]
                v.tensor_tensor(dst.rearrange("p a (h d) -> p (a h) d", h=H),
                                ps[:, 7, 0:D].rearrange("p (h d) -> p h d", h=H),
                                rinv[:, par, :].unsqueeze(2).broadcast_to((P, H, HD)), ALU.mult).then_inc(ctx_ready, 1)

            def dve_round(it, first, last):
                for k in range(UNITS):
                    ahead = not (last and k + AHEAD_QK >= UNITS)
                    for half in range(2):
                        if evacuated_by(k, 2 * half + 1) == "dve":
                            copy_out(it, k, 2 * half + 1)
                        if ahead:
                            mask_and_reduce(it, k + AHEAD_QK, half)
                    if (k + AHEAD_QK) % H == H - 1 and ahead:
                        wait(v, masked, 2 * (it * UNITS + k + AHEAD_QK) + 2)
                        v.sem_inc(mask_used, 1)
                    if k % H == 3 and not (first and k < 11):
                        normalise(it, k)

            for k in range(AHEAD_QK):
                if k == 2:
                    for hq in range(4):
                        v.wait_ge(stacked[hq], 16 * NG * 8)
                for half in range(2):
                    mask_and_reduce(0, k, half)
            rounds(v, dve_round)
            normalise(ROUNDS, 3)

            v.memset(sel_before, 0.0).then_inc(slot_step, 1)
            row = lambda i: rows_sb[:, i, :].unsqueeze(1).broadcast_to((P, GT, D))
            tiles = lambda c: slice(c * GT, (c + 1) * GT)

            def attention_residual(c):
                step, base = c * A_STEPS, c * LN_CHUNK
                nm = nmask[:, tiles(c)].unsqueeze(2).broadcast_to((P, GT, D))
                wait(v, attn_step, step)
                v.wait_ge(wo_psum, c + 1)
                v.tensor_tensor(u_c, ps[:, 2:4, :].rearrange("p b (j d) -> p (b j) d", j=2), row(3), ALU.add)\
                    .then_inc(attn_step, 1)
                v.wait_ge(attn_step, step + 1)
                v.tensor_tensor(u_c, u_c, nm, ALU.mult).then_inc(attn_step, 1)
                v.wait_ge(attn_step, step + 2)
                v.tensor_tensor(u_c, u_c, ht[:, tiles(c), :], ALU.add).then_inc(attn_step, 1)
                v.wait_ge(attn_step, step + 3)
                for j in range(GT):
                    v.bn_stats(stats[:, j, :], u_c[:, j, :]).then_inc(ln2_step, 1)
                v.wait_ge(ln2_step, base + GT)
                moments(v, GT, stats[:, 0:GT, :], base + GT, ln2_step)
                inverse_root(v, GT, base + GT, sqrt2, c + 1, ln2_step)
                for j in range(GT):
                    v.tensor_scalar(u_c[:, j, :], u_c[:, j, :], mean[:, j:j + 1], rstd[:, j:j + 1],
                                    ALU.subtract, ALU.mult).then_inc(attn_step, 1)
                v.wait_ge(attn_step, step + 7)
                v.tensor_tensor(u_c, u_c, row(4), ALU.mult).then_inc(attn_step, 1)
                v.wait_ge(attn_step, step + 8)
                v.tensor_tensor(u_c, u_c, row(5), ALU.add).then_inc(attn_step, 1)
                v.wait_ge(attn_step, step + 9)
                v.tensor_tensor(u_c, u_c, nm, ALU.mult).then_inc(u_ready, 1)
                if c == 0:
                    v.wait_ge(x2_in, 16)
                v.wait_ge(u_ready, c + 1)
                v.tensor_tensor(x2[:, tiles(c), :], x2[:, tiles(c), :], u_c, ALU.add).then_inc(attn_step, 1)

            def ffn_residual(c):
                base = c * LN_CHUNK
                v.wait_ge(attn_step, (c + 1) * A_STEPS)
                v.wait_ge(y_psum, c + 1)
                v.tensor_tensor(x2[:, tiles(c), :], ps[:, 4:6, :].rearrange("p b (j d) -> p (b j) d", j=2),
                                x2[:, tiles(c), :], ALU.add).then_inc(y_out, 1)
                v.wait_ge(y_out, c + 1)
                for j in range(GT):
                    v.bn_stats(stats[:, j, :], x2[:, c * GT + j, :]).then_inc(ln3_step, 1)
                v.wait_ge(ln3_step, base + GT)
                moments(v, GT, stats[:, 0:GT, :], base + GT, ln3_step)
                inverse_root(v, GT, base + GT, sqrt3, c + 1, ln3_step)
                for j in range(GT):
                    v.tensor_scalar(vals[:, c * GT + j, :], x2[:, c * GT + j, :], mean[:, j:j + 1],
                                    rstd[:, j:j + 1], ALU.subtract, ALU.mult).then_inc(xn3_ready, 1)

            def rank_experts(c):
                step = c * RANK_STEPS
                g = gates[:, tiles(c), :]
                v.wait_ge(gate_psum, c + 1)
                v.tensor_copy(g, ps[:, 2, 0:GT * E].rearrange("p (j e) -> p j e", j=GT)).then_inc(gate_out, 1)
                v.wait_ge(gate_out, c + 1)
                others, own = g.unsqueeze(2).broadcast_to((P, GT, E, E)), g.unsqueeze(3).broadcast_to((P, GT, E, E))
                v.tensor_tensor(larger, others, own, ALU.is_gt).then_inc(rank_step, 1)
                v.tensor_tensor(same, others, own, ALU.is_equal).then_inc(rank_step, 1)
                v.wait_ge(rank_step, step + 2)
                v.tensor_tensor(same, same, lower[:, :, :].unsqueeze(1).broadcast_to((P, GT, E, E)), ALU.mult)\
                    .then_inc(rank_step, 1)
                v.wait_ge(rank_step, step + 3)
                v.tensor_tensor(larger, larger, same, ALU.add).then_inc(rank_step, 1)
                v.wait_ge(rank_step, step + 4)
                v.tensor_reduce(rank[:, tiles(c), :], larger, AX_X, ALU.add).then_inc(rank_step, 1)
                v.wait_ge(rank_step, step + 5)
                v.tensor_scalar(sel[:, tiles(c), :], rank[:, tiles(c), :], 2.0, None, ALU.is_lt).then_inc(sel_ready, 1)

            def choose_slots(c):
                step = 1 + c * SLOT_STEPS
                p = pos[:, tiles(c), :]
                start = first_slot[:, :].unsqueeze(1).broadcast_to((P, GT, E))
                per_choice = lambda a: a.unsqueeze(2).broadcast_to((P, GT, 2, E))
                v.wait_ge(pos_psum, c + 1)
                v.tensor_copy(p, ps[:, 3, 0:GT * E].rearrange("p (j e) -> p j e", j=GT)).then_inc(pos_out, 1)
                v.wait_ge(pos_out, c + 1)
                v.tensor_scalar(from_slot, p, float(CAP - 1), None, ALU.min).then_inc(slot_step, 1)
                v.tensor_scalar(over, p, float(CAP), FAR, ALU.is_ge, ALU.mult).then_inc(slot_step, 1)
                v.tensor_tensor(to_slot, p, start, ALU.add).then_inc(slot_step, 1)
                v.tensor_tensor(pick, per_choice(rank[:, tiles(c), :]), choice[:, :, :].unsqueeze(1).broadcast_to((P, GT, 2, E)),
                                ALU.is_equal).then_inc(slot_step, 1)
                v.tensor_reduce(chunk_sel, sel[:, tiles(c), :].rearrange("p t e -> p e t"), AX_X, ALU.add)\
                    .then_inc(slot_step, 1)
                v.wait_ge(slot_step, step + 5)
                v.tensor_tensor(from_slot, from_slot, start, ALU.add).then_inc(slot_step, 1)
                v.tensor_tensor(to_slot, to_slot, over, ALU.add).then_inc(slot_step, 1)
                v.tensor_tensor(sel_before, sel_before, chunk_sel, ALU.add).then_inc(slot_step, 1)
                v.wait_ge(slot_step, step + 8)
                v.tensor_tensor(prod_in, pick, per_choice(from_slot), ALU.mult).then_inc(slot_step, 1)
                v.tensor_tensor(prod_out, pick, per_choice(to_slot), ALU.mult).then_inc(slot_step, 1)
                v.wait_ge(slot_step, step + 10)
                v.tensor_reduce(chosen_in, prod_in, AX_X, ALU.add).then_inc(slot_step, 1)
                v.tensor_reduce(chosen_out, prod_out, AX_X, ALU.add).then_inc(slot_step, 1)
                v.wait_ge(slot_step, step + 12)
                v.tensor_copy(idx_in[:, tiles(c), :], chosen_in).then_inc(slot_step, 1)
                v.tensor_copy(idx_out[:, tiles(c), :], chosen_out).then_inc(routed, 1)

            attention_residual(0)
            for c in range(NG):
                if c:
                    ffn_residual(c - 1)
                if c > 1:
                    choose_slots(c - 2)
                if c < NG - 1:
                    attention_residual(c + 1)
                if c:
                    rank_experts(c - 1)
            ffn_residual(NG - 1)
            choose_slots(NG - 2)
            rank_experts(NG - 1)
            choose_slots(NG - 1)

            count = [0]

            def link(ins):
                count[0] += 1
                ins.then_inc(weight_step, 1)
                v.wait_ge(weight_step, count[0])

            b16 = lambda a: a.unsqueeze(2).broadcast_to((P, NT, E))
            link(v.tensor_reduce(top, gates, AX_X, ALU.max))
            link(v.tensor_tensor(z, gates, b16(top), ALU.subtract))
            v.wait_ge(gate_exp, 1)
            link(v.tensor_reduce(total, ex, AX_X, ALU.add))
            link(v.reciprocal(inv, total))
            link(v.tensor_tensor(w, ex, b16(inv), ALU.mult))
            link(v.tensor_tensor(w, w, sel, ALU.mult))
            link(v.tensor_reduce(total, w, AX_X, ALU.add))
            link(v.reciprocal(inv, total))
            link(v.tensor_tensor(w, w, b16(inv), ALU.mult))
            link(v.tensor_scalar(keep, pos, float(CAP), None, ALU.is_lt))
            link(v.tensor_tensor(w, w, keep, ALU.mult))
            for k in range(2):
                link(v.tensor_scalar(z, rank, float(k), None, ALU.is_equal))
                link(v.tensor_tensor(z, z, w, ALU.mult))
                link(v.tensor_reduce(weight[k], z, AX_X, ALU.add))

            @peeled(v, E // 2)
            def _(pair):
                for i in range(2):
                    e = pair * 2 + i
                    v.tensor_copy(b1_e[i], b1T[:, bass.ds(e * NFE, NFE)]).then_inc(b1_ready, 1)
                    v.wait_ge(b2_in[i], pair * 16 + 16)
                    wait(v, eo_stored[i], pair * 32)
                    v.wait_ge(eo_psum, e + 1)
                    v.tensor_tensor(eout[i][:, 0:2, :], ps[:, 6, :].rearrange("p (j d) -> p j d", j=2),
                                    b2_row[i].unsqueeze(1).broadcast_to((P, 2, D)), ALU.add).then_inc(eo_out, 1)
                    v.tensor_tensor(eout[i][0:ROWS[2], 2, :], ps[0:ROWS[2], 7, 0:D], b2_row[i][0:ROWS[2], :], ALU.add)\
                        .then_inc(eo_out, 1)
            for t in range(NT):
                if t % GT == 0:
                    v.wait_ge(gathered[t // GT], 32 * GT)
                v.scalar_tensor_tensor(out=x2[:, t, :], in0=got[0][:, t, :], scalar=weight[0][:, t:t + 1],
                                       in1=x2[:, t, :], op0=ALU.mult, op1=ALU.add).then_inc(mix_step, 1)
                v.wait_ge(mix_step, t + 1)
                v.scalar_tensor_tensor(out=x2[:, t, :], in0=got[1][:, t, :], scalar=weight[1][:, t:t + 1],
                                       in1=x2[:, t, :], op0=ALU.mult, op1=ALU.add).then_inc(mixed, 1)

        @block.tensor
        def _(pe):
            pe.wait_ge(consts, 7)
            pe.wait_ge(gp_step, 8)
            pe.wait_ge(prep_dve, 1)
            pe.transpose(ps[:, 0, 0:NT], nm_f[:, :], ident[0:NT, 0:NT]).then_inc(prep_pe, 1)
            for k in range(ND):
                last = pe.transpose(ps[:, 1, k * E:(k + 1) * E], gw_rows[:, k * P:(k + 1) * P], ident[0:E, 0:E])
            last.then_inc(prep_pe, 1)
            pe.transpose(ps[:, 2, 0:E * NFE], b1_rows[:, :], ident[0:E * NFE, 0:E * NFE]).then_inc(prep_pe, 1)

            def turn_group(src, banks, done):
                for k in range(ND):
                    for j in range(GT):
                        last = pe.transpose(ps[:, banks + k, j * P:(j + 1) * P], src[:, j, k * P:(k + 1) * P], ident[:, :])
                last.then_inc(done, 1)

            pe.wait_ge(w_in, 16 * 4)
            pe.wait_ge(prep_dve, 5)
            @peeled(pe, NG)
            def _(g):
                pe.wait_ge(ht_ready, g + 1)
                wait(pe, v_out, 2 * g)
                turn_group(ht_c, 0, htT_psum)
                pe.wait_ge(hs_ready, g + 1)
                turn_group(hs_c, 2, hsT_psum)
                for w, src, bank, ready, done, out_sem in ((0, htT, 4, htT_out, q_psum, q_out),
                                                           (1, hsT, 6, hsT_out, k_psum, k_out)):
                    pe.wait_ge(ready, g + 1)
                    wait(pe, out_sem, ND * g)
                    for c in range(ND):
                        for k in range(ND):
                            last = pe.matmul(ps[:, bank + c, :], wqkvo[:, w, k, c * P:(c + 1) * P], src[:, k, :],
                                             start=(k == 0), stop=(k == ND - 1))
                    last.then_inc(done, 1)
                for j in range(GT):
                    for k in range(ND):
                        last = pe.matmul(ps[:, j // 2, (j % 2) * D:(j % 2 + 1) * D], hsT[:, k, j * P:(j + 1) * P],
                                         wqkvo[:, 2, k, :], start=(k == 0), stop=(k == ND - 1))
                    if j % 2:
                        last.then_inc(v_psum, 1)

            def score(it, k, half):
                n, s = it * UNITS + k, k % UNITS
                if isinstance(n, int) and n < 4 and half == 0:
                    pe.wait_ge(stacked[n], 16 * NG * 8)
                wait(pe, masked, 2 * (n - 1) + half + 1)
                at = (it * 2 + k // H) * P
                q = qst[:, s % H, bass.ds(at, P)] if not isinstance(at, int) else qst[:, s % H, at:at + P]
                for c in range(2):
                    last = pe.matmul(ps[:, 2 * half + c, :], q, kst[:, s % H, (2 * half + c) * 512:(2 * half + c + 1) * 512],
                                     start=True, stop=True)
                last.then_inc(scores, 1)

            def turn(it, k, g):
                n = it * UNITS + k
                if g % 2 == 0:
                    wait(pe, exp_done, 2 * n + 1 + g // 2)
                pk, pg = (k, g - 2) if g >= 2 else (k - 1, g + 2)
                if not (isinstance(n, int) and n == 0 and g < 2):
                    by = evacuated_by(pk, pg)
                    wait(pe, evac[by], evac_count(by, it, pk, pg))
                for b in range(4):
                    s = 4 * g + b
                    last = pe.transpose(ps[:, 4 + g % 2, b * P:(b + 1) * P], logits[k % RING][:, s * P:(s + 1) * P], ident[:, :])
                last.then_inc(turned, 1)

            def contexts(it, k, half):
                n, h = it * UNITS + k, k % H
                if half == 0:
                    for by in ("act", "dve"):
                        wait(pe, evac[by], evac_count(by, it, k, 3))
                    if k % HG == 0:
                        wait(pe, part_out, it * (UNITS // HG) + k // HG)
                for s in range(8 * half, 8 * half + 8):
                    j = s % 4
                    last = pe.matmul(ps[j * HD:(j + 1) * HD, 6, (h % HG) * P:(h % HG + 1) * P],
                                     vals[:, s, h * HD:(h + 1) * HD], probsT[k % 2][:, s * P:(s + 1) * P],
                                     start=(s < 4), stop=(s >= 12))
                if half:
                    last.then_inc(pv_done, 1)

            def fold_parts(it, k):
                G, g2 = it * (UNITS // HG) + (k - 6) // HG, ((k - 6) // HG) % 2
                wait(pe, part_out, G + 1)
                if g2 == 0:
                    wait(pe, ctx_ready, it * 2 + (k - 6) // H)
                for h in range(HG):
                    at = (g2 * HG + h) * HD
                    last = pe.matmul(ps[:, 7, at:at + HD], ctx_part[:, h * P:(h + 1) * P], fold[:, :],
                                     start=True, stop=True)
                last.then_inc(folded, 1)

            def pe_round(it, first, last):
                for k in range(UNITS):
                    for half in range(2):
                        turn(it, k, 2 * half)
                        turn(it, k, 2 * half + 1)
                        if not (first and k == 0):
                            contexts(it, k - 1, half)
                        if not (last and k + AHEAD_QK >= UNITS):
                            score(it, k + AHEAD_QK, half)
                    if k % HG == 2 and not (first and k < 6):
                        fold_parts(it, k)

            pe.wait_ge(v_out, 2 * NG)
            for k in range(AHEAD_QK):
                for half in range(2):
                    score(0, k, half)
            rounds(pe, pe_round)
            contexts(ROUNDS, -1, 0)
            contexts(ROUNDS, -1, 1)
            fold_parts(ROUNDS, 2)

            def turn_chunk(src, done):
                for k in range(ND):
                    for j in range(GT):
                        last = pe.transpose(ps[:, k, j * P:(j + 1) * P], src[:, j, k * P:(k + 1) * P], ident[:, :])
                last.then_inc(done, 1)

            def turn_contexts(c):
                turn_chunk(xn[:, c * GT:(c + 1) * GT, :], cxT_psum)

            def project_contexts(c):
                pe.wait_ge(cxT_out, c + 1)
                wait(pe, pos_out, c - 2)
                for j in range(GT):
                    for k in range(ND):
                        last = pe.matmul(ps[:, 2 + j // 2, (j % 2) * D:(j % 2 + 1) * D], ctxT[:, k, j * P:(j + 1) * P],
                                         wqkvo[:, 3, k, :], start=(k == 0), stop=(k == ND - 1))
                last.then_inc(wo_psum, 1)

            def turn_norm3(c):
                pe.wait_ge(xn3_ready, c * GT + GT)
                turn_chunk(vals[:, c * GT:(c + 1) * GT, :], n3T_psum)

            def gate_logits(c):
                pe.wait_ge(n3T_out, c + 1)
                pe.wait_ge(attn_step, min(c + 2, NG - 1) * A_STEPS + 1)
                for j in range(GT):
                    for k in range(ND):
                        last = pe.matmul(ps[:, 2, j * E:(j + 1) * E], xn3T[:, k, j * P:(j + 1) * P], gwT[:, k, :],
                                         start=(k == 0), stop=(k == ND - 1))
                last.then_inc(gate_psum, 1)

            def queue_positions(c):
                pe.wait_ge(sel_ready, c + 1)
                s = sel[:, c * GT:(c + 1) * GT, :]
                pe.matmul(ps[:, 3, 0:GT * E], before[:, :], s, start=True, stop=False)
                for t in range(1, GT):
                    pe.matmul(ps[:, 3, t * E:GT * E].rearrange("p (t e) -> p t e", e=E), ones[:, :],
                              s[:, t - 1:t, :].broadcast_to((P, GT - t, E)), start=False, stop=False)
                pe.matmul(ps[:, 3, 0:GT * E].rearrange("p (t e) -> p t e", e=E), ones[:, :],
                          sel_before.unsqueeze(1).broadcast_to((P, GT, E)), start=False, stop=True).then_inc(pos_psum, 1)

            pe.wait_ge(ctx_ready, NT)
            turn_contexts(0)
            project_contexts(0)
            pe.wait_ge(w1_in, 16)
            for c in range(NG):
                pe.wait_ge(u_ready, c + 1)
                turn_chunk(u_c, uT_psum)
                pe.wait_ge(uT_out, c + 1)
                for f in range(NF):
                    if f == 2:
                        wait(pe, y_out, c)
                    if f > 3:
                        pe.wait_ge(h_out, c * NF + f - 3)
                    for k in range(ND):
                        last = pe.matmul(ps[:, 4 + (f + 2) % 4, :], w1_sb[:, k, f * P:(f + 1) * P], uT[:, k, :],
                                         start=(k == 0), stop=(k == ND - 1))
                    last.then_inc(h_psum, 1)
                    if f == 3 and c < NG - 1:
                        turn_contexts(c + 1)
                    if f == 3 and c > 1:
                        queue_positions(c - 2)
                if c < NG - 1:
                    project_contexts(c + 1)
                if c:
                    turn_norm3(c - 1)
                if c == 0:
                    pe.wait_ge(w2_in, 16)
                pe.wait_ge(h_out, c * NF + NF)
                for j in range(GT):
                    for f in range(NF):
                        last = pe.matmul(ps[:, 4 + j // 2, (j % 2) * D:(j % 2 + 1) * D], hid[:, f, j * P:(j + 1) * P],
                                         w2_sb[:, f, :], start=(f == 0), stop=(f == NF - 1))
                    if j == 1 and c:
                        gate_logits(c - 1)
                last.then_inc(y_psum, 1)
            queue_positions(NG - 2)
            turn_norm3(NG - 1)
            gate_logits(NG - 1)
            queue_positions(NG - 1)

            @peeled(pe, E // 2)
            def _(pair):
                for i in range(2):
                    e = pair * 2 + i
                    pe.wait_ge(xin_in[i], pair * 32 + 32)
                    for k in range(ND):
                        for j, r in enumerate(ROWS):
                            last = pe.transpose(ps[:, k, j * P:j * P + r], xin[i][0:r, j, k * P:(k + 1) * P], ident[0:r, 0:r])
                    last.then_inc(xinT_psum, 1)
                    pe.wait_ge(ew_in[i], pair * 32 + 32)
                    pe.wait_ge(xinT_out, e + 1)
                    for f in range(NFE):
                        wait(pe, eh_out, e * NFE + f - 3)
                        for k in range(ND):
                            last = pe.matmul(ps[:, 2 + f % 4, 0:CAP], ew1[i][:, k, f * P:(f + 1) * P], xinT[:, k, :],
                                             start=(k == 0), stop=(k == ND - 1))
                        last.then_inc(eh_psum, 1)
                    pe.wait_ge(eh_out, e * NFE + NFE)
                    wait(pe, eo_out, 2 * e)
                    for j, r in enumerate(ROWS):
                        dst = ps[:, 6, j * D:(j + 1) * D] if j < 2 else ps[0:r, 7, 0:D]
                        for f in range(NFE):
                            last = pe.matmul(dst, ehid[i][:, f, j * P:j * P + r], ew2[i][:, f, :],
                                             start=(f == 0), stop=(f == NFE - 1))
                    last.then_inc(eo_psum, 1)


_INS = ["x", "adj", "nodemask", "L0_gnn_h_target", "L0_gnn_ln1_scale", "L0_gnn_ln1_bias", "L0_gnn_Wq", "L0_gnn_bq",
        "L0_gnn_Wk", "L0_gnn_bk", "L0_gnn_Wv", "L0_gnn_bv", "L0_gnn_Wo", "L0_gnn_bo", "L0_gnn_ln2_scale",
        "L0_gnn_ln2_bias", "L0_gnn_W1", "L0_gnn_W2", "L0_ffn_gate_w", "L0_ffn_w1", "L0_ffn_b1", "L0_ffn_w2",
        "L0_ffn_b2"]


def kernel(**inputs):
    import numpy as np
    import concourse.bacc as bacc
    from concourse.bass_utils import run_bass_kernel_spmd as run

    nc = bacc.Bacc("TRN2", target_bir_lowering=False, num_devices=1)
    arrays, args = {}, []
    for name in _INS:
        a = np.ascontiguousarray(inputs[name])
        arrays[f"in_{name}"] = a
        args.append(nc.dram_tensor(f"in_{name}", a.shape, mybir.dt.from_np(a.dtype), kind="ExternalInput").ap())
    out = nc.dram_tensor("out", inputs["x"].shape, F32, kind="ExternalOutput").ap()
    build(nc, *args, out)
    r = run(nc, [arrays], core_ids=[0])
    return r.results[0]["out"]
```

```python
from contextlib import ExitStack

import concourse.bass as bass
import concourse.mybir as mybir

F32 = mybir.dt.float32
F16 = mybir.dt.float16
BF16 = mybir.dt.bfloat16
I32 = mybir.dt.int32
ALU = mybir.AluOpType
ACT = mybir.ActivationFunctionType
AX_X = mybir.AxisListType.X

P = 128
EPS = 1e-5
BIG = 1e30
AHEAD_QK = 3
RING = 4
UNITS = 16


def evacuated_by(k, g):
    return "act" if g in (0, 2) or (g == 1 and k % 4 == 0) else "dve"


def evac_count(engine, it, k, g):
    four = {"act": 9, "dve": 7}[engine]
    within = sum(evacuated_by(kk, gg) == engine
                 for kk in range(k % 4 + 1) for gg in range(4) if (kk, gg) <= (k % 4, g))
    return it * (four * UNITS // 4) + (k // 4) * four + within


def wait(eng, sem, value):
    if not isinstance(value, int) or value > 0:
        eng.wait_ge(sem, value)


def peeled(eng, n):
    def run(body):
        body(0)
        with eng.Fori(1, n) as i:
            body(i)
    return run


def hold(eng, sem, value, passed):
    wait(eng, sem, value)
    eng.sem_inc(passed, 1)


def build(nc, x, adj, nodemask, h_target, ln1_scale, ln1_bias, Wq, bq, Wk, bk, Wv, bv, Wo, bo,
          ln2_scale, ln2_bias, W1, W2, gate_w, w1, b1, w2, b2, out):
    N, D = x.shape
    H, HD = 8, D // 8
    NT = N // P
    ND = D // P
    F = W1.shape[1]
    NF = F // P
    E, NFE = w1.shape[0], w1.shape[2] // P
    CAP = -(-5 * N // (4 * E))
    SLOTS = E * CAP
    REST = CAP - 2 * P
    ROWS = [P, P, REST]
    NG = 4
    GT = NT // NG
    GW = GT * P
    ROUNDS = NT * H // UNITS
    HG = 4
    SCALE = 1.0 / float(HD) ** 0.5
    FAR = float(1 << 20)
    assert 2 * REST == P and D == 2 * P and GW == 512 and NT == 16 and 4 * HD == P and UNITS == 2 * H

    slots_in = nc.dram_tensor("slots_in", (SLOTS, D), F32, kind="Internal").ap()
    slot_row = nc.dram_tensor("slot_row", (SLOTS, 1), I32, kind="Internal").ap()
    choice_out = nc.dram_tensor("choice_out", (2 * N, D), F32, kind="Internal").ap()

    with ExitStack() as ctx:
        def sb(name, shape, dt=F32):
            return ctx.enter_context(nc.sbuf_tensor(name, shape, dt))

        def sem(name):
            return ctx.enter_context(nc.semaphore(name))

        ps = ctx.enter_context(nc.psum_tensor("ps", [P, 8, 512], F32))

        xn = sb("xn", [P, NT, D])
        ht = sb("ht", [P, NT, D])
        vals = sb("vals", [P, NT, D])
        keys_q_arena = sb("keys_q_arena", [P, 16384])
        work = sb("work", [P, 12800])
        wqkvo = sb("wqkvo", [P, 4, ND, D])
        w1_sb = sb("w1_sb", [P, ND, F])
        adj_sb = sb("adj_sb", [P, N], I32)
        mask_sb = [sb(f"mask{i}", [P, N], BF16) for i in range(2)]
        rows_sb = sb("rows_sb", [P, 6, D])
        ident = sb("ident", [P, P])
        fold = sb("fold", [P, HD])
        before = sb("before", [P, P])
        ones = sb("ones", [P, P])
        lower = sb("lower", [P, E, E])
        first_slot = sb("first_slot", [P, E])
        choice = sb("choice", [P, 2, E])
        cols = sb("cols", [P, 5, ND])
        row_of = sb("row_of", [P, NT, 2], I32)
        no_row = sb("no_row", [P, SLOTS // P], I32)
        slot_rows = sb("slot_rows", [P, E, 3], I32)
        half_rows = sb("half_rows", [P, E], I32)
        which_half = sb("which_half", [P, 1])
        nm_i = sb("nm_i", [NT, P], I32)
        nm_f = sb("nm_f", [NT, P])
        nmask = sb("nmask", [P, NT])
        gw_rows = sb("gw_rows", [E, D])
        gwT = sb("gwT", [P, ND, E])
        b1_rows = sb("b1_rows", [E * NFE, P])
        b1T = sb("b1T", [P, E * NFE])
        stats = sb("stats", [P, 2 * NT, 6])
        mean = sb("mean", [P, 2 * NT])
        tmpa = sb("tmpa", [P, 2 * NT])
        tmpb = sb("tmpb", [P, 2 * NT])
        vare = sb("vare", [P, 2 * NT])
        sdev = sb("sdev", [P, 2 * NT])
        rstd = sb("rstd", [P, 2 * NT])
        least = sb("least", [P, 2, UNITS])
        rowsum = sb("rowsum", [P, 2, UNITS])
        rows2 = sb("rows2", [P, 2, H])
        rinv = sb("rinv", [P, 2, H])

        def view(arena, at, words, dt=F32):
            a = arena[:, at:at + words]
            return a if dt == F32 else a.bitcast(dt)

        kst = view(keys_q_arena, 0, 8192, F16).rearrange("p (h n) -> p h n", h=H)
        qst = view(keys_q_arena, 8192, 8192, F16).rearrange("p (h n) -> p h n", h=H)
        turned_c = [view(work, 1024 * i, 1024).rearrange("p (k n) -> p k n", k=ND) for i in range(2)]
        masked_c = [view(work, 2048 + 1024 * i, 1024).rearrange("p (k n) -> p k n", k=ND) for i in range(2)]
        split = [view(work, 4096 + 2048 * i, 2048, F16).rearrange("p (k n) -> p k n", k=ND)
                 for i in range(4)]
        logits = [view(work, 2048 * i, 2048) for i in range(RING)]
        probsT = [view(work, 8192 + 2048 * i, 2048) for i in range(2)]
        ctx_part = view(work, 12288, 512)
        mask_row = w1_sb[:, :, :].rearrange("p k f -> p (k f)")

        x2 = view(keys_q_arena, 0, 4096).rearrange("p (t d) -> p t d", t=NT)
        w2_sb = view(keys_q_arena, 4096, 2048).rearrange("p (k d) -> p k d", k=NF)
        ctxT = view(keys_q_arena, 6144, 1024).rearrange("p (k n) -> p k n", k=ND)
        hid = view(keys_q_arena, 7168, 4096).rearrange("p (f n) -> p f n", f=NF)
        u_c = view(keys_q_arena, 11264, 1024).rearrange("p (j d) -> p j d", j=GT)
        uT = view(keys_q_arena, 12288, 1024).rearrange("p (k n) -> p k n", k=ND)
        xn3T = view(keys_q_arena, 13312, 1024).rearrange("p (k n) -> p k n", k=ND)
        gates, rank, sel, pos, z, ex, w, keep = (view(work, NT * E * i, NT * E).rearrange("p (t e) -> p t e", t=NT)
                                                 for i in range(8))
        larger_of, same_of = (view(work, 1024 + 256 * i, 256).rearrange("p (t a b) -> p t a b", t=GT, a=E) for i in range(2))
        pick, prod = (view(work, 1536 + 64 * i, 64).rearrange("p (t k e) -> p t k e", t=GT, k=2)
                      for i in range(2))
        to_slot, over = (view(work, 1728 + 32 * i, 32).rearrange("p (t e) -> p t e", t=GT) for i in range(2))
        chosen = view(work, 1824, 8).rearrange("p (t k) -> p t k", t=GT)
        chunk_sel, sel_before = (view(work, 1840 + 8 * i, 8) for i in range(2))
        top, total, inv = (view(work, 1856 + 16 * i, 16) for i in range(3))
        weight = [view(work, 1904 + 16 * i, 16) for i in range(2)]
        slot_of = view(work, 1936, 32, I32).rearrange("p (t k) -> p t k", t=NT)
        xin = [view(work, 2048 + 768 * i, 768).rearrange("p (j d) -> p j d", j=3) for i in range(2)]
        b2_row = [view(work, 3584 + 256 * i, 256) for i in range(2)]
        ew1 = [view(work, 4096 + 2048 * i, 2048).rearrange("p (k f) -> p k f", k=ND) for i in range(2)]
        ew2 = [view(work, 8192 + 2048 * i, 2048).rearrange("p (k d) -> p k d", k=NFE) for i in range(2)]
        b1_e = [view(work, 12288 + 8 * i, 8) for i in range(2)]
        xinT = view(keys_q_arena, 4096, 640).rearrange("p (k n) -> p k n", k=ND)
        ehid = [view(keys_q_arena, 4736 + 2560 * i, 2560).rearrange("p (f n) -> p f n", f=NFE)
                for i in range(2)]
        eout = [view(keys_q_arena, 9856 + 768 * i, 768).rearrange("p (j d) -> p j d", j=3) for i in range(2)]
        got = [a[:, :, :].rearrange("p (t k) d -> p t k d", k=2) for a in (xn, ht)]

        x_in = [sem(f"x_in{g}") for g in range(NG)]
        ht_in = [sem(f"ht_in{g}") for g in range(NG)]
        w_in, small_in, rows_in, mask_row_in, mask_row_ready, zero_done = map(
            sem, ("w_in", "small_in", "rows_in", "mask_row_in", "mask_row_ready", "zero_done"))
        consts, gp_step, zeros_set = map(sem, ("consts", "gp_step", "zeros_set"))
        ln_step, sqrt_done = sem("ln_step"), sem("sqrt_done")
        prep_dve, prep_pe = sem("prep_dve"), sem("prep_pe")
        norm_step, residual_step = sem("norm_step"), sem("residual_step")
        turned1, turned1_out, proj_psum, proj_masked, hi_out, lo_out = map(
            sem, ("turned1", "turned1_out", "proj_psum", "proj_masked", "hi_out", "lo_out"))
        v_psum, v_out = sem("v_psum"), sem("v_out")
        stacked = [sem(f"stacked{hq}") for hq in range(4)]
        adj_in, mask_ready, mask_used = sem("adj_in"), sem("mask_ready"), sem("mask_used")
        scores, masked = sem("scores"), sem("masked")
        exp_done, turned = sem("exp_done"), sem("turned")
        pool_passed, dve_passed, sp_passed = sem("pool_passed"), sem("dve_passed"), sem("sp_passed")
        evac = {"act": sem("evac_act"), "dve": sem("evac_dve")}
        pv_done, part_out, folded = sem("pv_done"), sem("part_out"), sem("folded")
        rinv_done, ctx_ready = sem("rinv_done"), sem("ctx_ready")
        w1_in, w2_in, x2_in = sem("w1_in"), sem("w2_in"), sem("x2_in")
        cxT_psum, cxT_out, wo_psum, attn_step, u_ready = map(
            sem, ("cxT_psum", "cxT_out", "wo_psum", "attn_step", "u_ready"))
        uT_psum, uT_out, h_psum, h_out, y_psum, y_out, xn3_ready = map(
            sem, ("uT_psum", "uT_out", "h_psum", "h_out", "y_psum", "y_out", "xn3_ready"))
        n3T_psum, n3T_out, gate_psum, gate_out = map(sem, ("n3T_psum", "n3T_out", "gate_psum", "gate_out"))
        ln2_step, ln3_step, sqrt2, sqrt3 = map(sem, ("ln2_step", "ln3_step", "sqrt2", "sqrt3"))
        rank_step, sel_ready, pos_psum, pos_out, slot_step = map(
            sem, ("rank_step", "sel_ready", "pos_psum", "pos_out", "slot_step"))
        weight_step, gate_exp = sem("weight_step"), sem("gate_exp")
        routed, scattered = sem("routed"), sem("scattered")
        ew_in, xin_in, b2_in, eo_stored = ([sem(f"{name}{i}") for i in range(2)]
                                           for name in ("ew_in", "xin_in", "b2_in", "eo_stored"))
        xinT_psum, xinT_out, eh_psum, eh_out, eo_psum, eo_out, b1_ready = map(
            sem, ("xinT_psum", "xinT_out", "eh_psum", "eh_out", "eo_psum", "eo_out", "b1_ready"))
        choices_in = [sem(f"choices_in{g}") for g in range(NG)]
        no_row_set, rows_cleared, choices_cleared, slot_rows_in = map(
            sem, ("no_row_set", "rows_cleared", "choices_cleared", "slot_rows_in"))
        rows_scattered, row_numbers, half_rows_ready = map(sem, ("rows_scattered", "row_numbers", "half_rows_ready"))
        mixed, mix_step, stored = sem("mixed"), sem("mix_step"), sem("stored")

        def moments(v, n, st, base, ln_step=ln_step):
            m, a, b, ve, r = mean[:, 0:n], tmpa[:, 0:n], tmpb[:, 0:n], vare[:, 0:n], rstd[:, 0:n]
            v.tensor_tensor(m, st[:, :, 1], st[:, :, 4], ALU.add).then_inc(ln_step, 1)
            v.tensor_tensor(a, st[:, :, 1], st[:, :, 4], ALU.subtract).then_inc(ln_step, 1)
            v.tensor_tensor(b, st[:, :, 2], st[:, :, 5], ALU.add).then_inc(ln_step, 1)
            v.wait_ge(ln_step, base + 3)
            v.tensor_scalar(m, m, 0.5, None, ALU.mult).then_inc(ln_step, 1)
            v.scalar_tensor_tensor(out=ve, in0=a, scalar=0.25, in1=a, op0=ALU.mult, op1=ALU.mult).then_inc(ln_step, 1)
            v.wait_ge(ln_step, base + 5)
            v.scalar_tensor_tensor(out=a, in0=b, scalar=1.0 / D, in1=ve, op0=ALU.mult, op1=ALU.add).then_inc(ln_step, 1)
            v.wait_ge(ln_step, base + 6)
            v.tensor_scalar(ve, a, EPS, None, ALU.add).then_inc(ln_step, 1)

        def inverse_root(v, n, base, root_sem, root_count, ln_step=ln_step):
            a, ve, r = tmpa[:, 0:n], vare[:, 0:n], rstd[:, 0:n]
            v.wait_ge(root_sem, root_count)
            v.reciprocal(r, sdev[:, 0:n]).then_inc(ln_step, 1)
            v.wait_ge(ln_step, base + 8)
            v.tensor_tensor(a, r, r, ALU.mult).then_inc(ln_step, 1)
            v.wait_ge(ln_step, base + 9)
            v.tensor_tensor(a, a, ve, ALU.mult).then_inc(ln_step, 1)
            v.wait_ge(ln_step, base + 10)
            v.tensor_scalar(a, a, -0.5, 1.5, ALU.mult, ALU.add).then_inc(ln_step, 1)
            v.wait_ge(ln_step, base + 11)
            v.tensor_tensor(r, r, a, ALU.mult).then_inc(ln_step, 1)
            v.wait_ge(ln_step, base + 12)

        LN_STEPS = 12
        LN_CHUNK = GT + LN_STEPS
        A_STEPS = 10
        PARTS = [(c * GT, (c + 1) * GT) for c in range(NG - 1)] + [(NT - GT, NT - GT // 2), (NT - GT // 2, NT)]
        RANK_STEPS = 5

        def slot_steps(p):
            return 1 + 8 * min(p, NG - 1) + 6 * max(p - NG + 1, 0)

        def norm3_steps(p):
            return PARTS[p][0] + LN_STEPS * p

        STACKS = 16 * 4 * 4
        NORM1 = NT + LN_STEPS

        def rounds(eng, body, n=ROUNDS):
            body(0, True, False)
            with eng.Fori(1, n - 1) as it:
                body(it, False, False)
            body(n - 1, False, True)

        block = ctx.enter_context(nc.Block())

        @block.sync
        def _(sp):
            def load_tiles(dst, src, arrived, g):
                sp.dma_start(dst[:, g * GT:(g + 1) * GT, :],
                             src[g * GW:(g + 1) * GW, :].rearrange("(j p) d -> p j d", p=P)).then_inc(arrived[g], 16)

            for g in range(NG):
                load_tiles(ht, h_target, ht_in, g)
            sp.dma_start(nm_i[:, :], nodemask.rearrange("(t p) -> t p", p=P)).then_inc(small_in, 16)
            sp.dma_start(gw_rows[:, :], gate_w[:, :]).then_inc(small_in, 16)
            sp.dma_start(b1_rows[:, :], b1.rearrange("e (f p) -> (e f) p", p=P)).then_inc(small_in, 16)
            for i, r in enumerate((bq, bk, ln1_scale, ln1_bias)):
                sp.dma_start(cols[:, i, :], r.rearrange("(c p) -> p c", p=P), allow_slow_non_contiguous=True).then_inc(small_in, 16)
            for i, w in enumerate((Wq, Wk, Wv, Wo)):
                sp.dma_start(wqkvo[:, i, :, :], w.rearrange("(k p) n -> p k n", p=P)).then_inc(w_in, 16)
            for g in range(NG):
                load_tiles(xn, x, x_in, g)
            sp.dma_start(mask_row.bitcast(I32), nodemask.partition_broadcast(P)).then_inc(mask_row_in, 16)
            for i, r in enumerate((ln1_scale, ln1_bias, bv, bo, ln2_scale, ln2_bias)):
                sp.dma_start(rows_sb[:, i, :], r.partition_broadcast(P)).then_inc(rows_in, 16)
            sp.dma_start(adj_sb[:, :], adj[0:P, :]).then_inc(adj_in, 16)
            sp.wait_ge(zeros_set, 1)
            zeros = slots_in.rearrange("(p r) d -> p (r d)", p=P)
            for at in range(0, SLOTS * D // P, N // 2):
                sp.dma_start(zeros[:, at:at + N // 2], mask_sb[1][:, :].bitcast(F32)).then_inc(zero_done, 16)
            sp.wait_ge(mask_ready, 1)
            sp.dma_start(adj_sb[:, :], adj[P:2 * P, :]).then_inc(adj_in, 16)

            def stack(dst, parts, hq, tokens):
                for slot, part in enumerate(parts):
                    sp.dma_start(dst[HD * slot:HD * (slot + 1), hq:H:4, tokens],
                                 split[part][HD * hq:HD * (hq + 1), :, tokens]).then_inc(stacked[hq], 16)

            for n in range(4):
                dst, parts = ((qst, (0, 0, 1, 1)), (kst, (2, 3, 2, 3)))[n // 2]
                tokens = slice((n % 2) * N // 2, (n % 2 + 1) * N // 2)
                sp.wait_ge(lo_out, 2 * ND * (n + 1))
                for hq in range(4):
                    stack(dst, parts, hq, tokens)

            sp.wait_ge(zero_done, 16 * (SLOTS * D // P // (N // 2)))
            sp.dma_start(choice_out[0:SLOTS, :], slots_in[:, :]).then_inc(choices_cleared, 16)
            sp.dma_start(choice_out[SLOTS:2 * N, :], slots_in[0:2 * N - SLOTS, :]).then_inc(choices_cleared, 16)
            sp.wait_ge(no_row_set, 1)
            sp.dma_start(slot_row.rearrange("(p r) o -> p (r o)", p=P), no_row[:, :]).then_inc(rows_cleared, 16)

            sp.dma_start(w1_sb[:, :, :], W1.rearrange("(k p) n -> p k n", p=P)).then_inc(w1_in, 16)
            with sp.Fori(2, NT) as t:
                sp.wait_ge(mask_ready, t)
                sp.dma_start(adj_sb[:, :], adj[bass.ds(t * P, P), :]).then_inc(adj_in, 16)

            sp.wait_ge(masked, 2 * NT * H)
            sp.dma_start(x2[:, :, :], x.rearrange("(t p) d -> p t d", p=P)).then_inc(x2_in, 16)
            sp.dma_start(w2_sb[:, :, :], W2.rearrange("(k p) n -> p k n", p=P)).then_inc(w2_in, 16)

            def load_weights(e, i):
                sp.dma_start(ew1[i], w1[bass.ds(e, 1), :, :].rearrange("e (k p) f -> p (e k) f", p=P)).then_inc(ew_in[i], 16)
                sp.dma_start(ew2[i], w2[bass.ds(e, 1), :, :].rearrange("e (k p) f -> p (e k) f", p=P)).then_inc(ew_in[i], 16)
                sp.dma_start(b2_row[i], b2[bass.ds(e, 1), :].rearrange("e d -> (e d)").partition_broadcast(P)).then_inc(b2_in[i], 16)

            def load_rows(e, i):
                sp.dma_start(xin[i][:, 0:2, :],
                             slots_in[bass.ds(e * CAP, 2 * P), :].rearrange("(j p) d -> p j d", p=P)).then_inc(xin_in[i], 16)
                sp.dma_start(xin[i][0:ROWS[2], 2, :],
                             slots_in[bass.ds(e * CAP + 2 * P, ROWS[2]), :]).then_inc(xin_in[i], 16)

            sp.wait_ge(ctx_ready, NT)
            load_weights(0, 0)
            load_weights(1, 1)
            sp.wait_ge(scattered, 16 * 2 * NT)
            load_rows(0, 0)
            load_rows(1, 1)
            sp.wait_ge(rows_scattered, 16 * 2 * NT)
            for j, part, first in ((0, slice(0, P), 0), (1, slice(0, P), P),
                                   (2, slice(0, REST), 2 * P), (2, slice(REST, P), 2 * P)):
                sp.dma_start(slot_rows[part, :, j],
                             slot_row.rearrange("(e c) o -> c (e o)", e=E)[first:first + part.stop - part.start, :],
                             allow_slow_non_contiguous=True).then_inc(slot_rows_in, 16)
            with sp.Fori(1, E // 2) as pair:
                for i in range(2):
                    hold(sp, eo_out, 6 * pair + 3 * i - 3, sp_passed)
                    load_rows(pair * 2 + i, i)
                    load_weights(pair * 2 + i, i)
            for i in range(2):
                sp.wait_ge(eo_stored[i], 16 * 3 * E // 2)
            for g in range(NG):
                at = g % 2 * GT
                sp.dma_start(got[g // 2][:, at:at + GT, :, :],
                             choice_out[2 * g * GW:2 * (g + 1) * GW, :].rearrange("(t p k) d -> p t k d", p=P, k=2))\
                    .then_inc(choices_in[g], 16)

            with sp.Fori(0, NG) as g:
                sp.wait_ge(mixed, GT * g + GT)
                sp.dma_start(out[bass.ds(g * GW, GW), :].rearrange("(j p) d -> p j d", p=P),
                             x2[:, bass.ds(g * GT, GT), :]).then_inc(stored, 16)
            sp.wait_ge(stored, 16 * NG)

        @block.gpsimd
        def _(pool):
            pool.memset(mask_sb[1][:, :], 0.0).then_inc(zeros_set, 1)
            pool.memset(no_row[:, :], 2 * N).then_inc(no_row_set, 1)
            pool.iota(row_of[:, :, :], [[2 * P, NT], [1, 2]], base=0, channel_multiplier=2).then_inc(row_numbers, 1)
            for k in range(2):
                pool.memset(choice[:, k, :], float(k)).then_inc(consts, 1)
            pool.memset(ident[:, :], 0.0).then_inc(gp_step, 1)
            pool.memset(fold[:, :], 0.0).then_inc(gp_step, 1)
            pool.memset(before[:, :], 1.0).then_inc(gp_step, 1)
            pool.memset(lower[:, :, :], 1.0).then_inc(gp_step, 1)
            pool.memset(ones[:, :], 1.0).then_inc(consts, 1)
            pool.iota(first_slot[:, :], [[CAP, E]], base=0, channel_multiplier=0,
                      allow_small_or_imprecise_dtypes=True).then_inc(consts, 1)
            pool.wait_ge(gp_step, 4)
            pool.affine_select(out=ident[:, :], in_=ident[:, :], compare_op=ALU.not_equal, fill=1.0,
                               base=0, pattern=[[-1, P]], channel_multiplier=1).then_inc(consts, 1)
            pool.affine_select(out=before[:, :], in_=before[:, :], compare_op=ALU.is_gt, fill=0.0,
                               base=0, pattern=[[1, P]], channel_multiplier=-1).then_inc(consts, 1)
            pool.affine_select(out=lower[:, :, :], in_=lower[:, :, :], compare_op=ALU.is_gt, fill=0.0,
                               base=0, pattern=[[1, E], [-1, E]], channel_multiplier=0).then_inc(consts, 1)
            for j in range(P // HD):
                pool.affine_select(out=fold[:, :], in_=fold[:, :], compare_op=ALU.not_equal, fill=1.0,
                                   base=-HD * j, pattern=[[-1, HD]], channel_multiplier=1).then_inc(gp_step, 1)
                pool.wait_ge(gp_step, 5 + j)
            pool.wait_ge(mask_row_in, 16)
            pool.tensor_scalar(mask_row, mask_row.bitcast(I32), 1.0, None, ALU.is_equal).then_inc(mask_row_ready, 1)
            for m in range(2):
                if m:
                    pool.wait_ge(zero_done, 16 * (SLOTS * D // P // (N // 2)))
                pool.wait_ge(adj_in, 16 * (m + 1))
                pool.tensor_scalar(mask_sb[m][:, :], adj_sb[:, :], 0.0, BIG, ALU.is_equal, ALU.mult).then_inc(mask_ready, 1)
            pool.wait_ge(rows_in, 16 * 6)
            pool.wait_ge(prep_dve, 3)
            pool.wait_ge(turned1, NG)
            with pool.Fori(0, NG) as g:
                t = ht[:, bass.ds(g * GT, GT), :]
                pool.tensor_tensor(t, t, rows_sb[:, 0, :].unsqueeze(1).broadcast_to((P, GT, D)), ALU.mult)\
                    .then_inc(residual_step, 1)
                hold(pool, residual_step, 3 * g + 1, pool_passed)
                pool.tensor_tensor(t, t, rows_sb[:, 1, :].unsqueeze(1).broadcast_to((P, GT, D)), ALU.add)\
                    .then_inc(residual_step, 1)
                hold(pool, residual_step, 3 * g + 2, pool_passed)
                pool.tensor_tensor(t, t, nmask[:, bass.ds(g * GT, GT)].unsqueeze(2).broadcast_to((P, GT, D)), ALU.mult)\
                    .then_inc(residual_step, 1)
            with pool.Fori(1, NT // 2) as pair:
                for m in range(2):
                    pool.wait_ge(adj_in, 32 * pair + 16 * m + 16)
                    hold(pool, mask_used, 2 * pair + m - 1, pool_passed)
                    pool.tensor_scalar(mask_sb[m][:, :], adj_sb[:, :], 0.0, BIG, ALU.is_equal, ALU.mult)\
                        .then_inc(mask_ready, 1)
            pool.wait_ge(choices_cleared, 32)
            pool.wait_ge(rows_cleared, 16)
            pool.wait_ge(row_numbers, 1)
            rows, ids = (slots_in, scattered), (slot_row, rows_scattered)
            for (dst, done), p in ((rows, 0), (ids, 0), (rows, 1), (ids, 1), (rows, 2), (rows, 3), (rows, 4),
                                   (ids, 2), (ids, 3), (ids, 4)):
                pool.wait_ge(routed, p + 1)
                for t in range(*PARTS[p]):
                    for k in range(2):
                        src = vals[:, t, :] if dst is slots_in else row_of[:, t, k:k + 1]
                        pool.indirect_dma_start(out=dst, out_offset=bass.IndirectOffsetOnAxis(slot_of[:, t, k:k + 1], 0),
                                                in_=src, in_offset=None, bounds_check=SLOTS - 1,
                                                oob_is_err=False).then_inc(done, 16)
            pool.wait_ge(half_rows_ready, 2)
            pool.wait_ge(slot_rows_in, 16 * 4)
            pool.tensor_scalar(half_rows[:, :], slot_rows[:, :, 2], 2.0, which_half[:, 0:1], ALU.mult, ALU.add)\
                .then_inc(half_rows_ready, 1)
            pool.wait_ge(half_rows_ready, 3)
            for e in range(E):
                pool.wait_ge(eo_out, 3 * e + 3)
                for j in range(2):
                    pool.indirect_dma_start(out=choice_out,
                                            out_offset=bass.IndirectOffsetOnAxis(slot_rows[:, e, j:j + 1], 0),
                                            in_=eout[e % 2][:, j, :], in_offset=None, bounds_check=2 * N - 1,
                                            oob_is_err=False).then_inc(eo_stored[e % 2], 16)
                pool.indirect_dma_start(out=choice_out.rearrange("r (h d) -> (r h) d", h=2),
                                        out_offset=bass.IndirectOffsetOnAxis(half_rows[:, e:e + 1], 0),
                                        in_=eout[e % 2][:, 2, 0:P], in_offset=None, bounds_check=4 * N - 1,
                                        oob_is_err=False).then_inc(eo_stored[e % 2], 16)

        @block.scalar
        def _(act):
            def first_root(i):
                act.wait_ge(ln_step, (NT + 7, NORM1 + NT + 7, NORM1 + NT + 17)[i])
                act.activation(sdev[:, 0:NT], vare[:, 0:NT], ACT.Sqrt).then_inc(sqrt_done, 1)

            def turned_group(n):
                act.wait_ge(turned1, n + 1)
                for c in range(ND):
                    act.activation(turned_c[n % 2][:, c, :], ps[:, 2 * (n % 2) + c, :], ACT.Identity,
                                   scale=cols[:, 2, c:c + 1], bias=cols[:, 3, c:c + 1]).then_inc(turned1_out, 1)

            def high_parts(n):
                g, of_keys = n % NG, n // NG
                act.wait_ge(proj_masked, n + 1)
                for c in range(ND):
                    bias = cols[:, 1 if of_keys else 4, c:c + 1]
                    act.activation(split[2 * of_keys][:, c, g * GW:(g + 1) * GW], masked_c[n % 2][:, c, :],
                                   ACT.Identity, bias=bias).then_inc(hi_out, 1)

            first_root(0)
            act.wait_ge(small_in, 16 * 7)
            act.wait_ge(prep_dve, 2)
            turned_group(0)
            turned_group(1)
            first_root(1)
            high_parts(0)
            first_root(2)
            turned_group(2)
            high_parts(1)
            turned_group(3)
            high_parts(2)
            for n in range(NG, 2 * NG):
                turned_group(n)
                high_parts(n - 1)
            high_parts(2 * NG - 1)

            def exponentials(it, k, half):
                n, s = it * UNITS + k, k % UNITS
                if half == 0:
                    wait(act, masked, 2 * n + 2)
                    if s % H == 0:
                        wait(act, ctx_ready, it * 2 + k // H - 1)
                part = logits[s % RING][:, half * 1024:(half + 1) * 1024]
                act.activation(part, part, ACT.Exp, bias=least[:, 1, s:s + 1], scale=-1.0,
                               accum_out=rowsum[:, half, s:s + 1]).then_inc(exp_done, 1)

            def copy_out(it, k, g):
                n = it * UNITS + k
                if g == 0:
                    wait(act, pv_done, n - 1)
                wait(act, turned, 4 * n + g + 1)
                act.activation(probsT[k % 2][:, g * 512:(g + 1) * 512], ps[:, 4 + g % 2, :], ACT.Copy)\
                   .then_inc(evac["act"], 1)

            def partial_contexts(it, k):
                G = it * (UNITS // HG) + (k - 5) // HG
                wait(act, pv_done, G * HG + HG)
                wait(act, folded, G)
                act.activation(ctx_part, ps[:, 6, :], ACT.Copy).then_inc(part_out, 1)

            def turned_contexts(c):
                act.wait_ge(cxT_psum, c + 1)
                act.activation(ctxT[:, :, :], ps[:, 0:2, :], ACT.Copy).then_inc(cxT_out, 1)

            def act_round(it, first, last):
                for k in range(UNITS):
                    if last and k == UNITS - 2:
                        turned_contexts(0)
                    if k % HG == 1 and not (first and k < 5):
                        partial_contexts(it, k)
                    for g in range(4):
                        if evacuated_by(k, g) == "act":
                            copy_out(it, k, g)
                        if g % 2 == 1 and not (last and k + 2 >= UNITS):
                            exponentials(it, k + 2, g // 2)

            for k in range(2):
                for half in range(2):
                    exponentials(0, k, half)
            for hq in range(4):
                act.wait_ge(stacked[hq], STACKS)
            rounds(act, act_round)
            partial_contexts(ROUNDS, 1)

            def root_of_norm2(c):
                act.wait_ge(ln2_step, c * LN_CHUNK + GT + 7)
                act.activation(sdev[:, 0:GT], vare[:, 0:GT], ACT.Sqrt).then_inc(sqrt2, 1)

            def root_of_norm3(p):
                n = PARTS[p][1] - PARTS[p][0]
                act.wait_ge(ln3_step, norm3_steps(p) + n + 7)
                act.activation(sdev[:, 0:n], vare[:, 0:n], ACT.Sqrt).then_inc(sqrt3, 1)

            def turned_norm3(p):
                a, b = PARTS[p]
                part = slice(a % GT * P, (a % GT + b - a) * P)
                act.wait_ge(n3T_psum, p + 1)
                act.activation(xn3T[:, :, part], ps[:, 0:2, part], ACT.Copy).then_inc(n3T_out, 1)

            turned_contexts(1)
            root_of_norm2(0)
            for c in range(NG):
                act.wait_ge(uT_psum, c + 1)
                act.activation(uT[:, :, :], ps[:, 0:2, :], ACT.Copy).then_inc(uT_out, 1)
                for f in range(NF):
                    act.wait_ge(h_psum, c * NF + f + 1)
                    act.activation(hid[:, f, :], ps[:, 4 + (f + 2) % 4, :], ACT.Gelu_apprx_tanh).then_inc(h_out, 1)
                    if f == 1 and c:
                        root_of_norm3(c - 1)
                    if f == 3 and 0 < c < NG - 1:
                        turned_contexts(c + 1)
                if c:
                    turned_norm3(c - 1)
                if c < NG - 1:
                    root_of_norm2(c + 1)
            for p in (NG - 1, NG):
                root_of_norm3(p)
                turned_norm3(p)

            act.wait_ge(weight_step, 2)
            act.activation(ex, z, ACT.Exp).then_inc(gate_exp, 1)

            with act.Fori(0, E // 2) as pair:
                for i in range(2):
                    act.wait_ge(xinT_psum, pair * 2 + i + 1)
                    act.activation(xinT[:, :, :], ps[:, 0:2, 0:CAP], ACT.Copy).then_inc(xinT_out, 1)
                    act.wait_ge(b1_ready, pair * 2 + i + 1)
                    for f in range(NFE):
                        act.wait_ge(eh_psum, (pair * 2 + i) * NFE + f + 1)
                        act.activation(ehid[i][:, f, :], ps[:, 2 + f % 4, 0:CAP], ACT.Gelu,
                                       bias=b1_e[i][:, f:f + 1]).then_inc(eh_out, 1)

        @block.vector
        def _(v):
            def row_stats(rows, arrived, count):
                for t in range(NT):
                    if arrived and t % GT == 0:
                        v.wait_ge(arrived[t // GT], 16)
                    v.bn_stats(stats[:, t, :], rows[:, t, :]).then_inc(ln_step, 1)
                v.wait_ge(ln_step, count + NT)

            def norm_rows(rows, g):
                for t in range(g * GT, (g + 1) * GT):
                    v.tensor_scalar(rows[:, t, :], rows[:, t, :], mean[:, t:t + 1], rstd[:, t:t + 1],
                                    ALU.subtract, ALU.mult).then_inc(norm_step, 1)

            def mask_group(n):
                g, bank = n % NG, 4 if n >= NG else 4 + 2 * (n % 2)
                if n == 0:
                    v.wait_ge(mask_row_ready, 1)
                v.wait_ge(proj_psum, n + 1)
                wait(v, lo_out, ND * (n - 1))
                v.tensor_tensor(masked_c[n % 2], ps[:, bank:bank + 2, :],
                                mask_row[:, g * GW:(g + 1) * GW].unsqueeze(1).broadcast_to((P, ND, GW)),
                                ALU.mult).then_inc(proj_masked, 1)

            def low_parts(n):
                g, of_keys = n % NG, n // NG
                v.wait_ge(proj_masked, n + 1)
                v.wait_ge(hi_out, ND * n + ND)
                for c in range(ND):
                    bias = cols[:, 1 if of_keys else 4, c:c + 1]
                    v.scalar_tensor_tensor(out=split[2 * of_keys + 1][:, c, g * GW:(g + 1) * GW],
                                           in0=masked_c[n % 2][:, c, :], scalar=bias,
                                           in1=split[2 * of_keys][:, c, g * GW:(g + 1) * GW],
                                           op0=ALU.add, op1=ALU.subtract).then_inc(lo_out, 1)

            def masked_values(g):
                v.wait_ge(v_psum, g + 1)
                for j in range(GT):
                    t = g * GT + j
                    v.scalar_tensor_tensor(out=vals[:, t, :], in0=ps[:, 6 + j // 2, (j % 2) * D:(j % 2 + 1) * D],
                                           scalar=nmask[:, t:t + 1], in1=rows_sb[:, 2, :],
                                           op0=ALU.mult, op1=ALU.add).then_inc(v_out, 1)

            row_stats(ht, ht_in, 0)
            moments(v, NT, stats[:, 0:NT, :], NT)
            v.wait_ge(small_in, 16 * 7)
            v.tensor_scalar(nm_f[:, :], nm_i[:, :], 1.0, None, ALU.is_equal).then_inc(prep_dve, 1)
            v.tensor_scalar(cols[:, 4, :], cols[:, 0, :], -SCALE, None, ALU.mult).then_inc(prep_dve, 1)
            inverse_root(v, NT, NT, sqrt_done, 1)
            for g in range(NG):
                norm_rows(ht, g)
            v.wait_ge(prep_pe, 1)
            v.tensor_copy(nmask[:, :], ps[:, 4, 0:NT]).then_inc(prep_dve, 1)
            v.wait_ge(prep_pe, 2)
            v.tensor_copy(gwT[:, :, :], ps[:, 5, 0:ND * E].rearrange("p (k e) -> p k e", k=ND)).then_inc(prep_dve, 1)
            v.wait_ge(prep_pe, 3)
            v.tensor_copy(b1T[:, :], ps[:, 6, 0:E * NFE]).then_inc(prep_dve, 1)
            v.wait_ge(w_in, 16 * 4)
            v.tensor_scalar(wqkvo[:, 0, :, :], wqkvo[:, 0, :, :], -SCALE, None, ALU.mult).then_inc(prep_dve, 1)
            row_stats(xn, x_in, NORM1)
            v.wait_ge(norm_step, NT)
            base = NORM1 + NT
            moments(v, NT, stats[:, 0:NT, :], base)
            v.tensor_copy(tmpb[:, 0:NT], tmpa[:, 0:NT]).then_inc(ln_step, 1)
            mask_group(0)
            inverse_root(v, NT, base + 1, sqrt_done, 2)
            v.tensor_copy(rstd[:, NT:2 * NT], rstd[:, 0:NT]).then_inc(ln_step, 1)
            v.tensor_tensor(tmpa[:, 0:NT], rstd[:, 0:NT], rstd[:, 0:NT], ALU.mult).then_inc(ln_step, 1)
            v.wait_ge(ln_step, base + 15)
            v.tensor_tensor(tmpa[:, 0:NT], tmpa[:, 0:NT], tmpb[:, 0:NT], ALU.mult).then_inc(ln_step, 1)
            v.wait_ge(ln_step, base + 16)
            v.tensor_scalar(vare[:, 0:NT], tmpa[:, 0:NT], EPS, None, ALU.add).then_inc(ln_step, 1)
            inverse_root(v, NT, base + 10, sqrt_done, 3)
            v.tensor_tensor(rstd[:, 0:NT], rstd[:, 0:NT], rstd[:, NT:2 * NT], ALU.mult).then_inc(ln_step, 1)
            v.wait_ge(ln_step, base + 23)
            for g in range(NG):
                norm_rows(xn, g)
                low_parts(g)
                if g < NG - 1:
                    mask_group(g + 1)
            for g in range(NG):
                mask_group(NG + g)
                low_parts(NG + g)
                if g == 0:
                    v.wait_ge(rows_in, 16 * 6)
                if g < NG - 2:
                    masked_values(g)
            masked_values(NG - 2)
            masked_values(NG - 1)

            def mask_and_reduce(it, k, half):
                n, s = it * UNITS + k, k % UNITS
                if half == 0:
                    wait(v, turned, 4 * (n - RING) + 4)
                    if s % H == 0:
                        wait(v, mask_ready, it * 2 + k // H + 1)
                else:
                    wait(v, masked, 2 * n + 1)
                hold(v, scores, 2 * n + half + 1, dve_passed)
                view3 = (lambda a: a[:, half * 1024:(half + 1) * 1024].rearrange("p (b n) -> p b n", b=2))
                v.tensor_tensor_reduce(
                    out=view3(logits[s % RING]), in0=ps[:, 2 * half:2 * half + 2, :],
                    in1=view3(mask_sb[s // H]), scale=1.0, scalar=3.0e38 if half == 0 else least[:, 0, s:s + 1],
                    op0=ALU.add, op1=ALU.min, accum_out=least[:, half, s:s + 1]).then_inc(masked, 1)

            def copy_out(it, k, g):
                n = it * UNITS + k
                wait(v, pv_done, n - 1)
                wait(v, turned, 4 * n + g + 1)
                v.tensor_copy(probsT[k % 2][:, g * 512:(g + 1) * 512], ps[:, 4 + g % 2, :]).then_inc(evac["dve"], 1)

            def normalise(it, k):
                t, par = it * 2 + (k - 11) // H, ((k - 11) // H) % 2
                wait(v, folded, 2 * t + 2)
                wait(v, exp_done, 2 * (8 * t + 8))
                v.tensor_tensor(rows2[:, par, :], rowsum[:, 0, par * H:par * H + H],
                                rowsum[:, 1, par * H:par * H + H], ALU.add).then_inc(rinv_done, 1)
                wait(v, rinv_done, 2 * t + 1)
                v.reciprocal(rinv[:, par, :], rows2[:, par, :]).then_inc(rinv_done, 1)
                wait(v, rinv_done, 2 * t + 2)
                dst = xn[:, bass.ds(t, 1), :] if not isinstance(t, int) else xn[:, t:t + 1, :]
                v.tensor_tensor(dst.rearrange("p a (h d) -> p (a h) d", h=H),
                                ps[:, 7, 0:D].rearrange("p (h d) -> p h d", h=H),
                                rinv[:, par, :].unsqueeze(2).broadcast_to((P, H, HD)), ALU.mult).then_inc(ctx_ready, 1)

            def dve_round(it, first, last):
                for k in range(UNITS):
                    ahead = not (last and k + AHEAD_QK >= UNITS)
                    for half in range(2):
                        if evacuated_by(k, 2 * half + 1) == "dve":
                            copy_out(it, k, 2 * half + 1)
                        if ahead:
                            mask_and_reduce(it, k + AHEAD_QK, half)
                    if (k + AHEAD_QK) % H == H - 1 and ahead:
                        wait(v, masked, 2 * (it * UNITS + k + AHEAD_QK) + 2)
                        v.sem_inc(mask_used, 1)
                    if k % H == 3 and not (first and k < 11):
                        normalise(it, k)

            for k in range(AHEAD_QK):
                if k == 2:
                    for hq in range(4):
                        v.wait_ge(stacked[hq], STACKS)
                for half in range(2):
                    mask_and_reduce(0, k, half)
            rounds(v, dve_round)

            row = lambda i: rows_sb[:, i, :].unsqueeze(1).broadcast_to((P, GT, D))
            tiles = lambda c: slice(c * GT, (c + 1) * GT)

            def attention_residual(c):
                step, base = c * A_STEPS, c * LN_CHUNK
                nm = nmask[:, tiles(c)].unsqueeze(2).broadcast_to((P, GT, D))
                wait(v, attn_step, step)
                wait(v, uT_psum, c)
                if c == 0:
                    v.wait_ge(residual_step, 3 * NG)
                v.wait_ge(wo_psum, c + 1)
                v.tensor_tensor(u_c, ps[:, 2:4, :].rearrange("p b (j d) -> p (b j) d", j=2), row(3), ALU.add)\
                    .then_inc(attn_step, 1)
                v.wait_ge(attn_step, step + 1)
                v.tensor_tensor(u_c, u_c, nm, ALU.mult).then_inc(attn_step, 1)
                v.wait_ge(attn_step, step + 2)
                v.tensor_tensor(u_c, u_c, ht[:, tiles(c), :], ALU.add).then_inc(attn_step, 1)
                v.wait_ge(attn_step, step + 3)
                for j in range(GT):
                    v.bn_stats(stats[:, j, :], u_c[:, j, :]).then_inc(ln2_step, 1)
                v.wait_ge(ln2_step, base + GT)
                moments(v, GT, stats[:, 0:GT, :], base + GT, ln2_step)
                inverse_root(v, GT, base + GT, sqrt2, c + 1, ln2_step)
                for j in range(GT):
                    v.tensor_scalar(u_c[:, j, :], u_c[:, j, :], mean[:, j:j + 1], rstd[:, j:j + 1],
                                    ALU.subtract, ALU.mult).then_inc(attn_step, 1)
                v.wait_ge(attn_step, step + 7)
                v.tensor_tensor(u_c, u_c, row(4), ALU.mult).then_inc(attn_step, 1)
                v.wait_ge(attn_step, step + 8)
                v.tensor_tensor(u_c, u_c, row(5), ALU.add).then_inc(attn_step, 1)
                v.wait_ge(attn_step, step + 9)
                v.tensor_tensor(u_c, u_c, nm, ALU.mult).then_inc(u_ready, 1)
                if c == 0:
                    v.wait_ge(x2_in, 16)
                v.wait_ge(u_ready, c + 1)
                v.tensor_tensor(x2[:, tiles(c), :], x2[:, tiles(c), :], u_c, ALU.add).then_inc(attn_step, 1)

            def ffn_residual(p):
                a, b = PARTS[p]
                n, base = b - a, norm3_steps(p)
                bank = 4 + a % GT // 2
                v.wait_ge(attn_step, (a // GT + 1) * A_STEPS)
                v.wait_ge(y_psum, p + 1)
                v.tensor_tensor(x2[:, a:b, :], ps[:, bank:bank + n // 2, :].rearrange("p b (j d) -> p (b j) d", j=2),
                                x2[:, a:b, :], ALU.add).then_inc(y_out, 1)
                v.wait_ge(y_out, p + 1)
                for t in range(a, b):
                    v.bn_stats(stats[:, t - a, :], x2[:, t, :]).then_inc(ln3_step, 1)
                v.wait_ge(ln3_step, base + n)
                moments(v, n, stats[:, 0:n, :], base + n, ln3_step)
                inverse_root(v, n, base + n, sqrt3, p + 1, ln3_step)
                for t in range(a, b):
                    v.tensor_scalar(vals[:, t, :], x2[:, t, :], mean[:, t - a:t - a + 1],
                                    rstd[:, t - a:t - a + 1], ALU.subtract, ALU.mult).then_inc(xn3_ready, 1)

            def rank_experts(p):
                a, b = PARTS[p]
                n, step = b - a, p * RANK_STEPS
                g, r = gates[:, a:b, :], rank[:, a:b, :]
                larger, same = (x[:, 0:n, :, :] for x in (larger_of, same_of))
                v.wait_ge(gate_psum, p + 1)
                v.tensor_copy(g, ps[:, 2, a % GT * E:(a % GT + n) * E].rearrange("p (j e) -> p j e", j=n)).then_inc(gate_out, 1)
                v.wait_ge(gate_out, p + 1)
                others, own = g.unsqueeze(2).broadcast_to((P, n, E, E)), g.unsqueeze(3).broadcast_to((P, n, E, E))
                v.tensor_tensor(larger, others, own, ALU.is_gt).then_inc(rank_step, 1)
                v.tensor_tensor(same, others, own, ALU.is_equal).then_inc(rank_step, 1)
                v.wait_ge(rank_step, step + 2)
                v.tensor_tensor(same, same, lower[:, :, :].unsqueeze(1).broadcast_to((P, n, E, E)), ALU.mult)\
                    .then_inc(rank_step, 1)
                v.wait_ge(rank_step, step + 3)
                v.tensor_tensor(larger, larger, same, ALU.add).then_inc(rank_step, 1)
                v.wait_ge(rank_step, step + 4)
                v.tensor_reduce(r, larger, AX_X, ALU.add).then_inc(rank_step, 1)
                v.wait_ge(rank_step, step + 5)
                v.tensor_scalar(sel[:, a:b, :], r, 2.0, None, ALU.is_lt).then_inc(sel_ready, 1)

            def choose_slots(p):
                a, b = PARTS[p]
                n, step = b - a, slot_steps(p)
                counted = p < NG - 1
                place, to, far = pos[:, a:b, :], to_slot[:, 0:n, :], over[:, 0:n, :]
                pk, pr, ch = pick[:, 0:n, :, :], prod[:, 0:n, :, :], chosen[:, 0:n, :]
                per_choice = lambda x: x.unsqueeze(2).broadcast_to((P, n, 2, E))
                v.wait_ge(pos_psum, p + 1)
                v.tensor_copy(place, ps[:, 3, a % GT * E:(a % GT + n) * E].rearrange("p (j e) -> p j e", j=n))\
                    .then_inc(pos_out, 1)
                v.wait_ge(pos_out, p + 1)
                v.tensor_scalar(far, place, float(CAP), FAR, ALU.is_ge, ALU.mult).then_inc(slot_step, 1)
                v.tensor_tensor(to, place, first_slot[:, :].unsqueeze(1).broadcast_to((P, n, E)), ALU.add).then_inc(slot_step, 1)
                v.tensor_tensor(pk, per_choice(rank[:, a:b, :]), choice[:, :, :].unsqueeze(1).broadcast_to((P, n, 2, E)),
                                ALU.is_equal).then_inc(slot_step, 1)
                if counted:
                    v.tensor_reduce(chunk_sel, sel[:, a:b, :].rearrange("p t e -> p e t"), AX_X, ALU.add)\
                        .then_inc(slot_step, 1)
                v.wait_ge(slot_step, step + 3 + counted)
                v.tensor_tensor(to, to, far, ALU.add).then_inc(slot_step, 1)
                if counted:
                    v.tensor_tensor(sel_before, sel_before, chunk_sel, ALU.add).then_inc(slot_step, 1)
                v.wait_ge(slot_step, step + 4 + 2 * counted)
                v.tensor_tensor(pr, pk, per_choice(to), ALU.mult).then_inc(slot_step, 1)
                v.wait_ge(slot_step, step + 5 + 2 * counted)
                v.tensor_reduce(ch, pr, AX_X, ALU.add).then_inc(slot_step, 1)
                v.wait_ge(slot_step, step + 6 + 2 * counted)
                v.tensor_copy(slot_of[:, a:b, :], ch).then_inc(routed, 1)

            attention_residual(0)
            normalise(ROUNDS, 3)
            v.memset(sel_before, 0.0).then_inc(slot_step, 1)
            for c in range(NG):
                if c:
                    ffn_residual(c - 1)
                if c > 1:
                    choose_slots(c - 2)
                if c < NG - 1:
                    attention_residual(c + 1)
                if c:
                    rank_experts(c - 1)
            ffn_residual(NG - 1)
            choose_slots(NG - 2)
            ffn_residual(NG)
            for p in (NG - 1, NG):
                rank_experts(p)
                choose_slots(p)

            count = [0]

            def link(ins):
                count[0] += 1
                ins.then_inc(weight_step, 1)
                v.wait_ge(weight_step, count[0])

            b16 = lambda a: a.unsqueeze(2).broadcast_to((P, NT, E))
            link(v.tensor_reduce(top, gates, AX_X, ALU.max))
            link(v.tensor_tensor(z, gates, b16(top), ALU.subtract))
            v.wait_ge(gate_exp, 1)
            link(v.tensor_reduce(total, ex, AX_X, ALU.add))
            link(v.reciprocal(inv, total))
            link(v.tensor_tensor(w, ex, b16(inv), ALU.mult))
            link(v.tensor_tensor(w, w, sel, ALU.mult))
            link(v.tensor_reduce(total, w, AX_X, ALU.add))
            link(v.reciprocal(inv, total))
            link(v.tensor_tensor(w, w, b16(inv), ALU.mult))
            link(v.tensor_scalar(keep, pos, float(CAP), None, ALU.is_lt))
            link(v.tensor_tensor(w, w, keep, ALU.mult))
            for k in range(2):
                link(v.tensor_scalar(z, rank, float(k), None, ALU.is_equal))
                link(v.tensor_tensor(z, z, w, ALU.mult))
                link(v.tensor_reduce(weight[k], z, AX_X, ALU.add))

            for h in range(2):
                v.memset(which_half[h * REST:(h + 1) * REST, :], float(h)).then_inc(half_rows_ready, 1)

            @peeled(v, E // 2)
            def _(pair):
                for i in range(2):
                    e = pair * 2 + i
                    v.tensor_copy(b1_e[i], b1T[:, bass.ds(e * NFE, NFE)]).then_inc(b1_ready, 1)
                    v.wait_ge(b2_in[i], pair * 16 + 16)
                    wait(v, eo_stored[i], pair * 48)
                    v.wait_ge(eo_psum, e + 1)
                    v.tensor_tensor(eout[i][:, 0:2, :], ps[:, 6, :].rearrange("p (j d) -> p j d", j=2),
                                    b2_row[i].unsqueeze(1).broadcast_to((P, 2, D)), ALU.add).then_inc(eo_out, 1)
                    for h in range(2):
                        part = slice(h * REST, (h + 1) * REST)
                        v.tensor_tensor(eout[i][part, 2, 0:P], ps[part, 7, 0:P], b2_row[i][part, h * P:(h + 1) * P], ALU.add)\
                            .then_inc(eo_out, 1)
            for g in range(NG):
                v.wait_ge(choices_in[g], 16)
                for k in range(2):
                    counted = (mix_step, mixed)[k]
                    for t in range(g * GT, (g + 1) * GT):
                        if k == 1:
                            v.wait_ge(mix_step, t + 1)
                        v.scalar_tensor_tensor(out=x2[:, t, :], in0=got[t // 8][:, t % 8, k, :], scalar=weight[k][:, t:t + 1],
                                               in1=x2[:, t, :], op0=ALU.mult, op1=ALU.add).then_inc(counted, 1)

        @block.tensor
        def _(pe):
            pe.wait_ge(consts, 7)
            pe.wait_ge(gp_step, 8)
            pe.wait_ge(prep_dve, 1)
            pe.transpose(ps[:, 4, 0:NT], nm_f[:, :], ident[0:NT, 0:NT]).then_inc(prep_pe, 1)
            for k in range(ND):
                last = pe.transpose(ps[:, 5, k * E:(k + 1) * E], gw_rows[:, k * P:(k + 1) * P], ident[0:E, 0:E])
            last.then_inc(prep_pe, 1)
            pe.transpose(ps[:, 6, 0:E * NFE], b1_rows[:, :], ident[0:E * NFE, 0:E * NFE]).then_inc(prep_pe, 1)

            def turn_rows_of(src, g, bank, done):
                for k in range(ND):
                    for j in range(GT):
                        last = pe.transpose(ps[:, bank + k, j * P:(j + 1) * P], src[:, g * GT + j, k * P:(k + 1) * P], ident[:, :])
                last.then_inc(done, 1)

            def turn_normed(n):
                src, g = (ht, n) if n < NG else (xn, n - NG)
                pe.wait_ge(norm_step, GT * (n + 1))
                wait(pe, turned1_out, ND * (n - 1))
                turn_rows_of(src, g, 2 * (n % 2), turned1)

            def project(n):
                w, bank = (0, 4 + 2 * (n % 2)) if n < NG else (1, 4)
                pe.wait_ge(turned1_out, ND * n + ND)
                wait(pe, proj_masked, n - 1 if n < NG else n)
                for c in range(ND):
                    for k in range(ND):
                        last = pe.matmul(ps[:, bank + c, :], wqkvo[:, w, k, c * P:(c + 1) * P], turned_c[n % 2][:, k, :],
                                         start=(k == 0), stop=(k == ND - 1))
                last.then_inc(proj_psum, 1)

            def project_values(g):
                wait(pe, v_out, GT * g)
                for j in range(GT):
                    for k in range(ND):
                        last = pe.matmul(ps[:, 6 + j // 2, (j % 2) * D:(j % 2 + 1) * D],
                                         turned_c[g % 2][:, k, j * P:(j + 1) * P], wqkvo[:, 2, k, :],
                                         start=(k == 0), stop=(k == ND - 1))
                last.then_inc(v_psum, 1)

            turn_normed(0)
            turn_normed(1)
            pe.wait_ge(prep_dve, 6)
            project(0)
            turn_normed(2)
            project(1)
            turn_normed(3)
            project(2)
            project(3)
            turn_normed(NG)
            for n in range(NG, 2 * NG):
                if n < 2 * NG - 1:
                    turn_normed(n + 1)
                project(n)
                if n < 2 * NG - 2:
                    project_values(n - NG)
            project_values(NG - 2)
            project_values(NG - 1)

            def score(it, k, half):
                n, s = it * UNITS + k, k % UNITS
                if isinstance(n, int) and n < 4 and half == 0:
                    pe.wait_ge(stacked[n], STACKS)
                wait(pe, masked, 2 * (n - 1) + half + 1)
                at = (it * 2 + k // H) * P
                q = qst[:, s % H, bass.ds(at, P)] if not isinstance(at, int) else qst[:, s % H, at:at + P]
                for c in range(2):
                    last = pe.matmul(ps[:, 2 * half + c, :], q, kst[:, s % H, (2 * half + c) * 512:(2 * half + c + 1) * 512],
                                     start=True, stop=True)
                last.then_inc(scores, 1)

            def turn(it, k, g):
                n = it * UNITS + k
                if g % 2 == 0:
                    wait(pe, exp_done, 2 * n + 1 + g // 2)
                pk, pg = (k, g - 2) if g >= 2 else (k - 1, g + 2)
                if not (isinstance(n, int) and n == 0 and g < 2):
                    by = evacuated_by(pk, pg)
                    wait(pe, evac[by], evac_count(by, it, pk, pg))
                for b in range(4):
                    s = 4 * g + b
                    last = pe.transpose(ps[:, 4 + g % 2, b * P:(b + 1) * P], logits[k % RING][:, s * P:(s + 1) * P], ident[:, :])
                last.then_inc(turned, 1)

            def contexts(it, k, half):
                n, h = it * UNITS + k, k % H
                if half == 0:
                    for by in ("act", "dve"):
                        wait(pe, evac[by], evac_count(by, it, k, 3))
                    if k % HG == 0:
                        wait(pe, part_out, it * (UNITS // HG) + k // HG)
                for s in range(8 * half, 8 * half + 8):
                    j = s % 4
                    last = pe.matmul(ps[j * HD:(j + 1) * HD, 6, (h % HG) * P:(h % HG + 1) * P],
                                     vals[:, s, h * HD:(h + 1) * HD], probsT[k % 2][:, s * P:(s + 1) * P],
                                     start=(s < 4), stop=(s >= 12))
                if half:
                    last.then_inc(pv_done, 1)

            def fold_parts(it, k):
                G, g2 = it * (UNITS // HG) + (k - 6) // HG, ((k - 6) // HG) % 2
                wait(pe, part_out, G + 1)
                if g2 == 0:
                    wait(pe, ctx_ready, it * 2 + (k - 6) // H)
                for h in range(HG):
                    at = (g2 * HG + h) * HD
                    last = pe.matmul(ps[:, 7, at:at + HD], ctx_part[:, h * P:(h + 1) * P], fold[:, :],
                                     start=True, stop=True)
                last.then_inc(folded, 1)

            def turn_chunk(src, done):
                for k in range(ND):
                    for j in range(GT):
                        last = pe.transpose(ps[:, k, j * P:(j + 1) * P], src[:, j, k * P:(k + 1) * P], ident[:, :])
                last.then_inc(done, 1)

            def turn_contexts(c):
                pe.wait_ge(ctx_ready, GT * c + GT)
                turn_chunk(xn[:, c * GT:(c + 1) * GT, :], cxT_psum)

            def project_contexts(c):
                pe.wait_ge(cxT_out, c + 1)
                wait(pe, pos_out, c - 2)
                for j in range(GT):
                    for k in range(ND):
                        last = pe.matmul(ps[:, 2 + j // 2, (j % 2) * D:(j % 2 + 1) * D], ctxT[:, k, j * P:(j + 1) * P],
                                         wqkvo[:, 3, k, :], start=(k == 0), stop=(k == ND - 1))
                last.then_inc(wo_psum, 1)

            def pe_round(it, first, last):
                for k in range(UNITS):
                    for half in range(2):
                        turn(it, k, 2 * half)
                        turn(it, k, 2 * half + 1)
                        if not (first and k == 0):
                            contexts(it, k - 1, half)
                        if not (last and k + AHEAD_QK >= UNITS):
                            score(it, k + AHEAD_QK, half)
                    if k % HG == 2 and not (first and k < 6):
                        fold_parts(it, k)
                    if last and k == UNITS - 3:
                        pe.wait_ge(masked, 2 * NT * H)
                        turn_contexts(0)
                    if last and k == UNITS - 2:
                        project_contexts(0)

            pe.wait_ge(v_out, NT)
            for k in range(AHEAD_QK):
                for half in range(2):
                    score(0, k, half)
            rounds(pe, pe_round)
            contexts(ROUNDS, -1, 0)
            contexts(ROUNDS, -1, 1)
            fold_parts(ROUNDS, 2)

            def turn_norm3(p):
                a, b = PARTS[p]
                pe.wait_ge(xn3_ready, b)
                wait(pe, n3T_out, p)
                for k in range(ND):
                    for t in range(a, b):
                        last = pe.transpose(ps[:, k, t % GT * P:(t % GT + 1) * P], vals[:, t, k * P:(k + 1) * P], ident[:, :])
                last.then_inc(n3T_psum, 1)

            def gate_logits(p):
                a, b = PARTS[p]
                pe.wait_ge(n3T_out, p + 1)
                wait(pe, gate_out, p)
                pe.wait_ge(attn_step, min(a // GT + 2, NG - 1) * A_STEPS + 1)
                for t in range(a, b):
                    j = t % GT
                    for k in range(ND):
                        last = pe.matmul(ps[:, 2, j * E:(j + 1) * E], xn3T[:, k, j * P:(j + 1) * P], gwT[:, k, :],
                                         start=(k == 0), stop=(k == ND - 1))
                last.then_inc(gate_psum, 1)

            def queue_positions(p):
                a, b = PARTS[p]
                first = a // GT * GT
                out_of = lambda t: ps[:, 3, t % GT * E:(t % GT + b - t) * E].rearrange("p (t e) -> p t e", e=E)
                pe.wait_ge(sel_ready, p + 1)
                wait(pe, pos_out, p)
                pe.matmul(out_of(a), before[:, :], sel[:, a:b, :], start=True, stop=False)
                for t in range(first, b - 1):
                    to = max(t + 1, a)
                    pe.matmul(out_of(to), ones[:, :], sel[:, t:t + 1, :].broadcast_to((P, b - to, E)),
                              start=False, stop=False)
                pe.matmul(out_of(a), ones[:, :], sel_before.unsqueeze(1).broadcast_to((P, b - a, E)),
                          start=False, stop=True).then_inc(pos_psum, 1)

            turn_contexts(1)
            pe.wait_ge(attn_step, 1)
            project_contexts(1)
            pe.wait_ge(w1_in, 16)
            pe.wait_ge(ctx_ready, NT)
            for c in range(NG):
                pe.wait_ge(u_ready, c + 1)
                turn_chunk(u_c, uT_psum)
                pe.wait_ge(uT_out, c + 1)
                for f in range(NF):
                    if f == 2:
                        wait(pe, y_out, c)
                    if f > 3:
                        pe.wait_ge(h_out, c * NF + f - 3)
                    for k in range(ND):
                        last = pe.matmul(ps[:, 4 + (f + 2) % 4, :], w1_sb[:, k, f * P:(f + 1) * P], uT[:, k, :],
                                         start=(k == 0), stop=(k == ND - 1))
                    last.then_inc(h_psum, 1)
                    if f == 3 and 0 < c < NG - 1:
                        turn_contexts(c + 1)
                    if f == 3 and c > 1:
                        queue_positions(c - 2)
                if 0 < c < NG - 1:
                    project_contexts(c + 1)
                if c:
                    turn_norm3(c - 1)
                if c == 0:
                    pe.wait_ge(w2_in, 16)
                pe.wait_ge(h_out, c * NF + NF)
                for j in range(GT):
                    for f in range(NF):
                        last = pe.matmul(ps[:, 4 + j // 2, (j % 2) * D:(j % 2 + 1) * D], hid[:, f, j * P:(j + 1) * P],
                                         w2_sb[:, f, :], start=(f == 0), stop=(f == NF - 1))
                    if j == 1 and c == NG - 1:
                        last.then_inc(y_psum, 1)
                    if j == 1 and c:
                        gate_logits(c - 1)
                    if j == 2 and c == NG - 1:
                        queue_positions(NG - 2)
                last.then_inc(y_psum, 1)
            turn_norm3(NG - 1)
            gate_logits(NG - 1)
            turn_norm3(NG)
            queue_positions(NG - 1)
            gate_logits(NG)
            queue_positions(NG)

            def turn_rows(e, i):
                pe.wait_ge(xin_in[i], 32 * (e // 2) + 32 if isinstance(e, int) else 16 * (e - i) + 32)
                for k in range(ND):
                    for j, r in enumerate(ROWS):
                        last = pe.transpose(ps[:, k, j * P:j * P + r], xin[i][0:r, j, k * P:(k + 1) * P], ident[0:r, 0:r])
                last.then_inc(xinT_psum, 1)

            def expert_pair(pair, first, final):
                for i in range(2):
                    e = pair * 2 + i
                    pe.wait_ge(ew_in[i], pair * 32 + 32)
                    pe.wait_ge(xinT_out, e + 1)
                    for f in range(NFE):
                        wait(pe, eh_out, e * NFE + f - 3)
                        for k in range(ND):
                            last = pe.matmul(ps[:, 2 + f % 4, 0:CAP], ew1[i][:, k, f * P:(f + 1) * P], xinT[:, k, :],
                                             start=(k == 0), stop=(k == ND - 1))
                        last.then_inc(eh_psum, 1)
                    if not (final and i == 1):
                        turn_rows(e + 1, 1 - i)
                    pe.wait_ge(eh_out, e * NFE + NFE)
                    wait(pe, eo_out, 3 * e)
                    for j in range(2):
                        for f in range(NFE):
                            pe.matmul(ps[:, 6, j * D:(j + 1) * D], ehid[i][:, f, j * P:(j + 1) * P], ew2[i][:, f, :],
                                      start=(f == 0), stop=(f == NFE - 1))
                    for f in range(NFE):
                        for h in range(2):
                            last = pe.matmul(ps[h * REST:(h + 1) * REST, 7, 0:P], ehid[i][:, f, 2 * P:CAP],
                                             ew2[i][:, f, h * P:(h + 1) * P], start=(f == 0), stop=(f == NFE - 1))
                    last.then_inc(eo_psum, 1)

            turn_rows(0, 0)
            rounds(pe, expert_pair, E // 2)


_INS = ["x", "adj", "nodemask", "L0_gnn_h_target", "L0_gnn_ln1_scale", "L0_gnn_ln1_bias", "L0_gnn_Wq", "L0_gnn_bq",
        "L0_gnn_Wk", "L0_gnn_bk", "L0_gnn_Wv", "L0_gnn_bv", "L0_gnn_Wo", "L0_gnn_bo", "L0_gnn_ln2_scale",
        "L0_gnn_ln2_bias", "L0_gnn_W1", "L0_gnn_W2", "L0_ffn_gate_w", "L0_ffn_w1", "L0_ffn_b1", "L0_ffn_w2",
        "L0_ffn_b2"]


def kernel(**inputs):
    import numpy as np
    import concourse.bacc as bacc
    from concourse.bass_utils import run_bass_kernel_spmd as run

    nc = bacc.Bacc("TRN2", target_bir_lowering=False, num_devices=1)
    arrays, args = {}, []
    for name in _INS:
        a = np.ascontiguousarray(inputs[name])
        arrays[f"in_{name}"] = a
        args.append(nc.dram_tensor(f"in_{name}", a.shape, mybir.dt.from_np(a.dtype), kind="ExternalInput").ap())
    out = nc.dram_tensor("out", inputs["x"].shape, F32, kind="ExternalOutput").ap()
    build(nc, *args, out)
    r = run(nc, [arrays], core_ids=[0])
    return r.results[0]["out"]
```
